# Optimizing a Trainium2 kernel written in Bass

```python
import numpy as np
import jax
import jax.numpy as jnp

def _softmax(x, axis=-1):
    return jax.nn.softmax(x, axis=axis)

def _gelu(x):
    return jax.nn.gelu(x, approximate=True)

def _silu(x):
    return jax.nn.silu(x)

def _sigmoid(x):
    return jax.nn.sigmoid(x)

def _layernorm(x, axis=-1, eps=1e-05):
    m = jnp.mean(x, axis=axis, keepdims=True)
    v = jnp.var(x, axis=axis, keepdims=True)
    return (x - m) / jnp.sqrt(v + eps)

def _scatter_add(tgt, idx, src, axis=0):
    return tgt.at[idx].add(src)

def _segment_sum(src, seg, n):
    return jax.ops.segment_sum(src, seg, n)
kernel_name = 'mk_seq_preln_d1_jaxref_r8_139307'

def setup_inputs(seed: int=0):
    np.random.seed(seed)
    _w = jnp.asarray

    def _L0_attn_setup():
        import jax, jax.numpy as jnp
        import numpy as np
        from math import ceil
        DIM = 128
        D_STATE = 16
        D_CONV = 4
        EXPAND = 2
        DI = DIM * EXPAND
        DT_RANK = ceil(DIM / 16)

        def _mamba(x, W_in, W_conv, b_conv, W_xproj, W_dt, b_dt, A_log, D, W_out):
            b, l, _ = x.shape
            silu = jax.nn.silu
            xr = x @ W_in.T
            xc, res = (xr[..., :DI], xr[..., DI:])
            u = jnp.transpose(xc, (0, 2, 1))
            u = jax.lax.conv_general_dilated(u, W_conv, window_strides=(1,), padding=[(D_CONV - 1, 0)], dimension_numbers=('NCH', 'OIH', 'NCH'), feature_group_count=DI)
            u = silu(u + b_conv[None, :, None])
            x_dbl = jnp.einsum('bdl,ed->ble', u, W_xproj)
            dt = x_dbl[..., :DT_RANK]
            B = x_dbl[..., DT_RANK:DT_RANK + D_STATE]
            C = x_dbl[..., DT_RANK + D_STATE:]
            delta = jax.nn.softplus(dt @ W_dt.T + b_dt)
            A = -jnp.exp(A_log)
            dA = jnp.exp(jnp.einsum('bld,dn->lbdn', delta, A))
            dBu = jnp.einsum('bld,bln,bdl->lbdn', delta, B, u)
            Cl = jnp.transpose(C, (1, 0, 2))

            def step(h, inp):
                dA_t, dBu_t, c_t = inp
                h = dA_t * h + dBu_t
                return (h, jnp.einsum('bdn,bn->bd', h, c_t))
            h0 = jnp.zeros((b, DI, D_STATE), u.dtype)
            _, ys = jax.lax.scan(step, h0, (dA, dBu, Cl))
            y = jnp.transpose(ys, (1, 2, 0)) + u * D[None, :, None]
            y = jnp.transpose(y, (0, 2, 1)) * silu(res)
            return y @ W_out.T
        key = jax.random.key(seed)
        ks = jax.random.split(key, 8)
        b, l = (2, 128)
        sc = lambda k, shp, s=0.02: jax.random.normal(k, shp, jnp.float32) * s
        x = jax.random.normal(ks[0], (b, l, DIM), jnp.float32)
        W_in = sc(ks[1], (2 * DI, DIM))
        W_conv = sc(ks[2], (DI, 1, D_CONV), 0.1)
        b_conv = jnp.zeros((DI,), jnp.float32)
        W_xproj = sc(ks[3], (DT_RANK + 2 * D_STATE, DI))
        W_dt = sc(ks[4], (DI, DT_RANK), 0.1)
        b_dt = jnp.zeros((DI,), jnp.float32)
        A_log = jnp.log(jnp.tile(jnp.arange(1, D_STATE + 1, dtype=jnp.float32)[None, :], (DI, 1)))
        D = jnp.ones((DI,), jnp.float32)
        W_out = sc(ks[5], (DIM, DI))
        return dict(x=x, W_in=W_in, W_conv=W_conv, b_conv=b_conv, W_xproj=W_xproj, W_dt=W_dt, b_dt=b_dt, A_log=A_log, D=D, W_out=W_out)
    _L0_attn_in = _L0_attn_setup()

    def _L0_ffn_setup():
        import jax, jax.numpy as jnp
        import numpy as np
        DIM = 128
        HIDDEN = 384
        SCALE = 1.0 / 127.0

        def _dequant(w_int, dtype):
            return w_int.astype(dtype) * jnp.asarray(SCALE, dtype)
        key = jax.random.key(seed)
        k_x, k_g, k_u, k_d = jax.random.split(key, 4)
        x = jax.random.normal(k_x, (4, 256, DIM), dtype=jnp.float32)
        w_gate = jax.random.randint(k_g, (HIDDEN, DIM), -127, 128, dtype=jnp.int32)
        w_up = jax.random.randint(k_u, (HIDDEN, DIM), -127, 128, dtype=jnp.int32)
        w_down = jax.random.randint(k_d, (DIM, HIDDEN), -127, 128, dtype=jnp.int32)
        return {'x': x, 'w_gate': w_gate, 'w_up': w_up, 'w_down': w_down}
    _L0_ffn_in = _L0_ffn_setup()
    _d = {'L0_attn_x': _L0_attn_in['x'], 'L0_attn_W_in': _L0_attn_in['W_in'], 'L0_attn_W_conv': _L0_attn_in['W_conv'], 'L0_attn_b_conv': _L0_attn_in['b_conv'], 'L0_attn_W_xproj': _L0_attn_in['W_xproj'], 'L0_attn_W_dt': _L0_attn_in['W_dt'], 'L0_attn_b_dt': _L0_attn_in['b_dt'], 'L0_attn_A_log': _L0_attn_in['A_log'], 'L0_attn_D': _L0_attn_in['D'], 'L0_attn_W_out': _L0_attn_in['W_out'], 'L0_ffn_w_gate': _L0_ffn_in['w_gate'], 'L0_ffn_w_up': _L0_ffn_in['w_up'], 'L0_ffn_w_down': _L0_ffn_in['w_down']}
    _x0 = _d['L0_attn_x']
    _d['L0_attn_x'] = jax.random.normal(jax.random.fold_in(jax.random.key(seed), 1), (8, 1024, 128), dtype=_x0.dtype)
    del _x0
    return _d

def reference(L0_attn_x, L0_attn_W_in, L0_attn_W_conv, L0_attn_b_conv, L0_attn_W_xproj, L0_attn_W_dt, L0_attn_b_dt, L0_attn_A_log, L0_attn_D, L0_attn_W_out, L0_ffn_w_gate, L0_ffn_w_up, L0_ffn_w_down):

    def _L0_attn_ref(x, W_in, W_conv, b_conv, W_xproj, W_dt, b_dt, A_log, D, W_out):
        import jax, jax.numpy as jnp
        import numpy as np
        from math import ceil
        DIM = 128
        D_STATE = 16
        D_CONV = 4
        EXPAND = 2
        DI = DIM * EXPAND
        DT_RANK = ceil(DIM / 16)

        def _mamba(x, W_in, W_conv, b_conv, W_xproj, W_dt, b_dt, A_log, D, W_out):
            b, l, _ = x.shape
            silu = jax.nn.silu
            xr = x @ W_in.T
            xc, res = (xr[..., :DI], xr[..., DI:])
            u = jnp.transpose(xc, (0, 2, 1))
            u = jax.lax.conv_general_dilated(u, W_conv, window_strides=(1,), padding=[(D_CONV - 1, 0)], dimension_numbers=('NCH', 'OIH', 'NCH'), feature_group_count=DI)
            u = silu(u + b_conv[None, :, None])
            x_dbl = jnp.einsum('bdl,ed->ble', u, W_xproj)
            dt = x_dbl[..., :DT_RANK]
            B = x_dbl[..., DT_RANK:DT_RANK + D_STATE]
            C = x_dbl[..., DT_RANK + D_STATE:]
            delta = jax.nn.softplus(dt @ W_dt.T + b_dt)
            A = -jnp.exp(A_log)
            dA = jnp.exp(jnp.einsum('bld,dn->lbdn', delta, A))
            dBu = jnp.einsum('bld,bln,bdl->lbdn', delta, B, u)
            Cl = jnp.transpose(C, (1, 0, 2))

            def step(h, inp):
                dA_t, dBu_t, c_t = inp
                h = dA_t * h + dBu_t
                return (h, jnp.einsum('bdn,bn->bd', h, c_t))
            h0 = jnp.zeros((b, DI, D_STATE), u.dtype)
            _, ys = jax.lax.scan(step, h0, (dA, dBu, Cl))
            y = jnp.transpose(ys, (1, 2, 0)) + u * D[None, :, None]
            y = jnp.transpose(y, (0, 2, 1)) * silu(res)
            return y @ W_out.T
        return _mamba(x, W_in, W_conv, b_conv, W_xproj, W_dt, b_dt, A_log, D, W_out)

    def _L0_ffn_ref(x, w_gate, w_up, w_down):
        import jax, jax.numpy as jnp
        import numpy as np
        DIM = 128
        HIDDEN = 384
        SCALE = 1.0 / 127.0

        def _dequant(w_int, dtype):
            return w_int.astype(dtype) * jnp.asarray(SCALE, dtype)
        wg = _dequant(w_gate, x.dtype)
        wu = _dequant(w_up, x.dtype)
        wd = _dequant(w_down, x.dtype)
        gate = jnp.einsum('bsd,hd->bsh', x, wg)
        up = jnp.einsum('bsd,hd->bsh', x, wu)
        h = jax.nn.silu(gate) * up
        return jnp.einsum('bsh,dh->bsd', h, wd)
    x = L0_attn_x
    x = x + _L0_attn_ref(_layernorm(x, axis=-1), L0_attn_W_in, L0_attn_W_conv, L0_attn_b_conv, L0_attn_W_xproj, L0_attn_W_dt, L0_attn_b_dt, L0_attn_A_log, L0_attn_D, L0_attn_W_out)
    x = x + _L0_ffn_ref(_layernorm(x, axis=-1), L0_ffn_w_gate, L0_ffn_w_up, L0_ffn_w_down)
    return x

_drawn_inputs = setup_inputs


def setup_inputs(seed=0):
    import zlib

    import numpy as np

    out = dict(_drawn_inputs(seed))
    spreads = {'L0_attn_b_conv': (0.0, 0.8), 'L0_attn_b_dt': (0.0, 0.8), 'L0_attn_D': (1.0, 0.6)}
    factors = {'L0_attn_W_in': 8.0,
     'L0_attn_W_conv': 8.0,
     'L0_attn_W_xproj': 8.0,
     'L0_attn_W_dt': 8.0,
     'L0_attn_A_log': 8.0,
     'L0_attn_W_out': 8.0}
    for name, (base, spread) in spreads.items():
        noise = np.random.default_rng([zlib.crc32(name.encode()), seed]).standard_normal(out[name].shape)
        drawn = base * np.exp(spread * noise) if base else spread * noise
        out[name] = jnp.asarray(drawn.astype(out[name].dtype))
    for name, factor in factors.items():
        out[name] = (out[name] * factor).astype(out[name].dtype)
    return out
```

```python
import concourse.bass as bass
from concourse import mybir
from contextlib import ExitStack


def mamba_block_and_gated_ffn(
    nc: bass.Bass,
    x_in: bass.AP,
    W_in: bass.AP,
    W_conv: bass.AP,
    b_conv: bass.AP,
    W_xproj: bass.AP,
    W_dt: bass.AP,
    b_dt: bass.AP,
    A_log: bass.AP,
    D_skip: bass.AP,
    W_out: bass.AP,
    w_gate: bass.AP,
    w_up: bass.AP,
    w_down: bass.AP,
    out: bass.AP,
):
    fp32 = mybir.dt.float32
    bf16 = mybir.dt.bfloat16
    int32 = mybir.dt.int32
    ALU = mybir.AluOpType
    ACT = mybir.ActivationFunctionType

    BATCH, SEQ, DIM = x_in.shape
    DI = W_dt.shape[0]
    R = W_dt.shape[1]
    NS = A_log.shape[1]
    HID = w_gate.shape[0]
    TAPS = W_conv.shape[2]
    SCALE = 1.0 / 127.0
    EPS = 1e-5
    LN_SHIFT = 2.0 ** -22
    P = 128
    T = 512
    TT = T // P
    CPB = SEQ // T
    CHUNKS = BATCH * CPB
    DT = DI // P
    HT = HID // P
    GD = P // NS
    CB = 4
    QPT = P // 32 * 4 // CB
    QUADS = DT * QPT
    GROUPS = QUADS * CB
    PARTS = 3
    HALO = TAPS - 1
    RING = 4
    assert CPB == 2 and DIM == P and GD == 8 and QUADS == 8

    x_v = x_in.rearrange("b (c a p) d -> (b c) p a d", c=CPB, p=P)
    out_v = out.rearrange("b (c a p) d -> (b c) p a d", c=CPB, p=P)

    ctx = ExitStack()
    with ctx:
        def sb(name, shape, dt=fp32):
            return ctx.enter_context(nc.sbuf_tensor(name, shape, dt))

        def sem(name):
            return ctx.enter_context(nc.semaphore(name))

        CONV, RES, BW, CW, OW, GW, UW, DW = 0, 8, 10, 12, 14, 16, 19, 22
        NW = 25
        dbu = sb("dbu", [P, RING, CB, T])
        dbu_flat = dbu[:, :, :, :].rearrange("p r c t -> p (r c t)")
        w_rows = dbu_flat[:, 0:NW * P].rearrange("p (w m) -> p w m", m=P)
        w_int = dbu_flat[:, NW * P:(2 * NW - GW) * P].bitcast(int32).rearrange("p (w m) -> p w m", m=P)
        w_in_rows = sb("w_in_rows", [P, DT, P])
        conv_w = sb("conv_w", [P, DT, TAPS])
        alog_rows = sb("alog_rows", [GROUPS, P])
        wx_dt = sb("wx_dt", [R, DI])
        wdt_T = sb("wdt_T", [R, DI])
        bconv = sb("bconv", [P, DT])
        bdt = sb("bdt", [P, DT])
        dskip = sb("dskip", [P, DT])
        wT = sb("wT", [P, NW, P])
        w_delta = sb("w_delta", [P, DT, DI])
        a_exp = sb("a_exp", [P, GROUPS])
        a_neg = sb("a_neg", [P, GROUPS])
        ident = sb("ident", [P, P])
        sel = sb("sel", [P, QPT, PARTS, 32])
        rep = sb("rep", [PARTS * 32, QPT, P], bf16)
        eps_col = sb("eps_col", [P, 1])
        one_col = sb("one_col", [P, 1])
        zero_col = sb("zero_col", [P, 1])

        x_t = sb("x_t", [P, 2, TT, P])
        x_again = sb("x_again", [P, 2, TT, P])
        stats_seen = sb("stats_seen", [P, 1])
        stats1 = sb("stats1", [P, TT, 6])
        mv1 = sb("mv1", [P, TT, 2])
        lnv1 = sb("lnv1", [P, TT])
        rstd1 = sb("rstd1", [P, TT])
        xn = sb("xn", [P, TT, P])
        xT = sb("xT", [P, HALO + 1 + CPB * T])
        pre = sb("pre", [P, 2 * DT, T])
        u_res = sb("u_res", [P, 2, 2 * DT, T])
        b_rep = sb("b_rep", [P, 2, T])
        a_dt = sb("a_dt", [P, DT, T])
        relu_dt = sb("relu_dt", [P, DT, T])
        e_dt = sb("e_dt", [P, DT, T])
        s_dt = sb("s_dt", [P, DT, T])
        delta = sb("delta", [P, DT, T])
        rest = sb("rest", [P, DT, T])
        part = [sb(f"part{j}", [P, DT, T], bf16) for j in range(PARTS)]
        stack = sb("stack", [PARTS * 32, 2, CB, DT, T], bf16)
        du = sb("du", [P, 2, DT, T])
        h = sb("h", [P, 2, CB, T])
        carry = sb("carry", [P, QUADS, CB])
        hc = sb("hc", [P, 2, CB, T])
        y_skip = sb("y_skip", [P, T])
        y_gated = sb("y_gated", [P, DT, T])
        x2 = sb("x2", [P, TT, P])
        stats2 = sb("stats2", [P, TT, 6])
        mv2 = sb("mv2", [P, TT, 2])
        lnv2 = sb("lnv2", [P, TT])
        rstd2 = sb("rstd2", [P, TT])
        x2n = sb("x2n", [P, TT, P])
        x2T = sb("x2T", [P, T])
        ffn_h = sb("ffn_h", [P, HT, T])
        fin = sb("fin", [P, 2, TT, P])

        banks = [ctx.enter_context(nc.psum_tensor(f"bank{i}", [P, T], fp32)) for i in range(8)]
        dA = banks[0:4]
        c_bank, y_bank, w0, w1 = banks[4:8]

        weights_in = sem("weights_in")
        consts_set = sem("consts_set")
        sel_step = sem("sel_step")
        w_scaled = sem("w_scaled")
        wT_made = sem("wT_made")
        wT_kept = sem("wT_kept")
        wdelta_made = sem("wdelta_made")
        a_done = sem("a_done")
        setup_done = sem("setup_done")

        x_loaded = [sem(f"x_loaded{i}") for i in range(2)]
        x_reloaded = [sem(f"x_reloaded{i}") for i in range(2)]
        stats1_done = sem("stats1_done")
        mv1_done = sem("mv1_done")
        lnv1_done = sem("lnv1_done")
        rstd1_done = sem("rstd1_done")
        norm1_done = sem("norm1_done")
        xT_made = sem("xT_made")
        xT_kept = sem("xT_kept")
        pre_made = sem("pre_made")
        pre_kept = sem("pre_kept")
        u_done = sem("u_done")
        b_made = sem("b_made")
        b_kept = sem("b_kept")
        draw_made = sem("draw_made")
        dexp_done = sem("dexp_done")
        dabs_done = sem("dabs_done")
        dkept = sem("dkept")
        dfactor_done = sem("dfactor_done")
        dsquare_done = sem("dsquare_done")
        dseries_done = sem("dseries_done")
        dlog_done = sem("dlog_done")
        dln_done = sem("dln_done")
        delta_done = sem("delta_done")
        du_done = sem("du_done")
        part0_done = sem("part0_done")
        rest_done = sem("rest_done")
        part1_done = sem("part1_done")
        part2_done = sem("part2_done")
        stacked = [sem(f"stacked{i}") for i in range(2)]
        du_spread = [sem(f"du_spread{i}") for i in range(RING)]
        dbu_done = sem("dbu_done")
        delta_spread = sem("delta_spread")
        dA_done = sem("dA_done")
        c_made = sem("c_made")
        scan_done = sem("scan_done")
        carried = sem("carried")
        hc_done = sem("hc_done")
        sum_done = sem("sum_done")
        skip_done = sem("skip_done")
        y_done = sem("y_done")
        mix_made = sem("mix_made")
        x2_done = sem("x2_done")
        stats2_done = sem("stats2_done")
        mv2_done = sem("mv2_done")
        lnv2_done = sem("lnv2_done")
        rstd2_done = sem("rstd2_done")
        norm2_done = sem("norm2_done")
        x2T_made = sem("x2T_made")
        x2T_kept = sem("x2T_kept")
        gate_made = sem("gate_made")
        gate_kept = sem("gate_kept")
        gate_done = sem("gate_done")
        up_made = sem("up_made")
        ffn_h_done = sem("ffn_h_done")
        down_made = sem("down_made")
        fin_done = sem("fin_done")
        stored = [sem(f"stored{i}") for i in range(2)]

        block = ctx.enter_context(nc.Block())
        LOADS = 15

        def over_chunks(eng, chunk):
            def batch(b, first, last):
                for c in range(CPB):
                    chunk(b * CPB + c, b, c, not (last and c == CPB - 1), not last,
                          not (first and c == 0))
            batch(0, True, False)
            with eng.Fori(1, BATCH - 1) as b:
                batch(b, False, False)
            batch(BATCH - 1, False, True)

        def stack_count(k, par):
            return 8 * PARTS * CB * (k - par + 2)

        def x_count(k, par):
            return 8 * (k - par + 2)

        @block.sync
        def _(sp):
            sp.dma_start(w_in_rows[:, :, :], W_in[0:DI, :].rearrange("(t p) m -> p t m", p=P)).then_inc(weights_in, 16)
            sp.dma_start(w_rows[:, RES:RES + DT, :], W_in[DI:2 * DI, :].rearrange("(t p) m -> p t m", p=P)).then_inc(weights_in, 16)
            sp.dma_start(conv_w[:, :, :], W_conv.rearrange("(t p) o k -> p t (o k)", p=P)).then_inc(weights_in, 16)
            sp.dma_start(alog_rows[:, :], A_log.rearrange("(g l) n -> g (l n)", g=GROUPS)).then_inc(weights_in, 16)
            sp.dma_start(wx_dt[:, :], W_xproj[0:R, :]).then_inc(weights_in, 16)
            sp.dma_start(wdt_T[:, :], W_dt.rearrange("d r -> r d"), allow_slow_non_contiguous=True).then_inc(weights_in, 16)
            for col, vec in ((bconv, b_conv), (bdt, b_dt), (dskip, D_skip)):
                sp.dma_start(col[:, :], vec.rearrange("(t p) -> p t", p=P), allow_slow_non_contiguous=True).then_inc(weights_in, 16)
            for at, row in ((BW, R), (CW, R + NS)):
                rows = W_xproj[row:row + NS, :].rearrange("n (t m) -> n t m", t=DT)
                sp.dma_start(w_rows[:, at:at + DT, :], rows.unsqueeze(0).broadcast_to([GD, NS, DT, P])).then_inc(weights_in, 16)
            sp.dma_start(w_rows[:, OW:OW + DT, :], W_out.rearrange("m (t p) -> m t p", p=P)).then_inc(weights_in, 16)
            sp.dma_start(w_int[:, 0:HT, :], w_gate.rearrange("(t p) m -> p t m", p=P)).then_inc(weights_in, 16)
            sp.dma_start(w_int[:, HT:2 * HT, :], w_up.rearrange("(t p) m -> p t m", p=P)).then_inc(weights_in, 16)
            sp.dma_start(w_int[:, 2 * HT:3 * HT, :], w_down.rearrange("m (t p) -> m t p", p=P)).then_inc(weights_in, 16)

            def load_x(k, par):
                sp.dma_start(x_t[:, par, :, :], x_v[k, :, :, :]).then_inc(x_loaded[par], 16)

            def reload_x(k, par):
                sp.dma_start(x_again[:, par, :, :], x_v[k, :, :, :]).then_inc(x_reloaded[par], 16)

            def spread_du(par, q):
                tile, sub, slot = q // QPT, q % QPT, q % RING
                for c in range(CB):
                    row = 32 * c + GD * sub
                    sp.dma_start(dbu[:, slot, c, :],
                                 du[row:row + GD, par, tile, :].unsqueeze(1).broadcast_to([GD, NS, T]))\
                      .then_inc(du_spread[slot], 16)

            def stack_delta(par):
                for j in range(PARTS):
                    for c in range(CB):
                        sp.dma_start(stack[32 * j:32 * j + 32, par, c, :, :],
                                     part[j][32 * c:32 * c + 32, :, :]).then_inc(stacked[par], 16)

            load_x(0, 0)
            load_x(1, 1)
            sp.wait_ge(du_done, 1)
            spread_du(0, 0)
            spread_du(0, 1)
            sp.wait_ge(part2_done, 1)
            stack_delta(0)
            spread_du(0, 2)
            spread_du(0, 3)

            def chunk(k, b, par, has_next, has_after_next, has_previous):
                nxt = 1 - par
                if has_after_next:
                    sp.wait_ge(norm1_done, k + 1)
                    load_x(k + 2, par)
                if has_previous and not (isinstance(k, int) and k == 1):
                    sp.wait_ge(x2_done, k - 1)
                reload_x(k, par)
                for s in range(RING, QUADS):
                    sp.wait_ge(scan_done, GROUPS * k + CB * (s - RING + 1))
                    spread_du(par, s)
                if has_next:
                    sp.wait_ge(weights_in, 16 * LOADS)
                    sp.wait_ge(du_done, k + 2)
                    for s in range(2):
                        sp.wait_ge(scan_done, GROUPS * k + CB * (s + RING + 1))
                        spread_du(nxt, s)
                    sp.wait_ge(part2_done, k + 2)
                    stack_delta(nxt)
                    for s in range(2, RING):
                        sp.wait_ge(scan_done, GROUPS * k + CB * (s + RING + 1))
                        spread_du(nxt, s)
                if has_previous:
                    sp.wait_ge(fin_done, k)
                    sp.dma_start(out_v[k - 1, :, :, :], fin[:, nxt, :, :]).then_inc(stored[nxt], 16)

            over_chunks(sp, chunk)
            sp.wait_ge(fin_done, CHUNKS)
            sp.dma_start(out_v[CHUNKS - 1, :, :, :], fin[:, 1, :, :]).then_inc(stored[1], 16)
            for par in range(2):
                sp.wait_ge(stored[par], 16 * CHUNKS // 2)

        @block.gpsimd
        def _(pool):
            nc.gpsimd.memset(ident[:, :], 0.0).then_inc(sel_step, 1)
            nc.gpsimd.memset(sel[:, :, :, :], 1.0).then_inc(sel_step, 1)
            nc.gpsimd.memset(eps_col[:, :], EPS).then_inc(consts_set, 1)
            nc.gpsimd.memset(one_col[:, :], 1.0 + LN_SHIFT).then_inc(consts_set, 1)
            nc.gpsimd.memset(zero_col[:, :], 0.0).then_inc(consts_set, 1)
            nc.gpsimd.memset(xT[:, 0:HALO], 0.0).then_inc(consts_set, 1)
            pool.wait_ge(sel_step, 2)
            nc.gpsimd.affine_select(out=ident[:, :], in_=ident[:, :], compare_op=ALU.not_equal, fill=1.0,
                                    base=0, pattern=[[-1, P]], channel_multiplier=1).then_inc(consts_set, 1)
            nc.gpsimd.affine_select(out=sel[:, :, :, :], in_=sel[:, :, :, :], compare_op=ALU.is_ge, fill=0.0,
                                    base=0, pattern=[[P, QPT], [0, PARTS], [-NS, 32]], channel_multiplier=1)\
              .then_inc(sel_step, 1)
            pool.wait_ge(sel_step, 3)
            nc.gpsimd.affine_select(out=sel[:, :, :, :], in_=sel[:, :, :, :], compare_op=ALU.is_ge, fill=0.0,
                                    base=NS - 1, pattern=[[-P, QPT], [0, PARTS], [NS, 32]], channel_multiplier=-1)\
              .then_inc(consts_set, 1)

            def times_b(k, par, s, turn):
                slot = s % RING
                pool.wait_ge(du_spread[slot], 16 * CB * turn)
                if s == 0:
                    pool.wait_ge(b_kept, k + 1)
                nc.gpsimd.tensor_tensor(dbu[:, slot, :, :], dbu[:, slot, :, :],
                                        b_rep[:, par, :].unsqueeze(1).broadcast_to([P, CB, T]), ALU.mult)\
                  .then_inc(dbu_done, 1)

            def times_e(k):
                pool.wait_ge(dfactor_done, k + 1)
                nc.gpsimd.tensor_tensor(s_dt[:, :, :], s_dt[:, :, :], e_dt[:, :, :], ALU.mult).then_inc(dsquare_done, 1)

            def add_relu(k):
                pool.wait_ge(dlog_done, k + 1)
                if not (isinstance(k, int) and k < 1):
                    pool.wait_ge(part0_done, k)
                nc.gpsimd.tensor_tensor(delta[:, :, :], relu_dt[:, :, :], s_dt[:, :, :], ALU.add).then_inc(delta_done, 1)

            def times_u(k, par):
                pool.wait_ge(delta_done, k + 1)
                if not (isinstance(k, int) and k < 2):
                    pool.wait_ge(dbu_done, QUADS * (k - 1))
                nc.gpsimd.tensor_tensor(du[:, par, :, :], delta[:, :, :], u_res[:, par, 0:DT, :], ALU.mult)\
                  .then_inc(du_done, 1)

            def first_rest(k):
                pool.wait_ge(part0_done, k + 1)
                nc.gpsimd.tensor_tensor(rest[:, :, :], delta[:, :, :], part[0][:, :, :], ALU.subtract)\
                  .then_inc(rest_done, 1)

            def last_part(k, par):
                pool.wait_ge(part1_done, k + 1)
                if not (isinstance(k, int) and k < 1):
                    pool.wait_ge(stacked[1 - par], stack_count(k - 1, 1 - par))
                nc.gpsimd.tensor_tensor(part[2][:, :, :], rest[:, :, :], part[1][:, :, :], ALU.subtract)\
                  .then_inc(part2_done, 1)

            times_e(0)
            add_relu(0)
            times_u(0, 0)
            first_rest(0)
            last_part(0, 0)
            times_b(0, 0, 0, 1)

            def chunk(k, b, par, has_next, has_after_next, has_previous):
                for s in range(QUADS):
                    if s + 1 < QUADS:
                        times_b(k, par, s + 1, 2 * k + (s + 1) // RING + 1)
                    elif has_next:
                        times_b(k + 1, 1 - par, 0, 2 * k + 3)
                    if has_next and s == 4:
                        times_e(k + 1)
                    if has_next and s == 5:
                        add_relu(k + 1)
                        times_u(k + 1, 1 - par)
                        first_rest(k + 1)
                    if has_next and s == 6:
                        last_part(k + 1, 1 - par)

            over_chunks(pool, chunk)

        @block.scalar
        def _(act):
            act.wait_ge(consts_set, 6)
            act.wait_ge(wT_kept, 7)
            nc.scalar.activation(a_exp[:, :], a_exp[:, :], ACT.Exp).then_inc(a_done, 1)

            def exps(k, s):
                tile, sub = s // QPT, s % QPT
                for c in range(CB):
                    g = tile * QPT * CB + QPT * c + sub
                    act.wait_ge(delta_spread, GROUPS * k + CB * s + c + 1)
                    nc.scalar.activation(dA[c][:, :], dA[c][:, :], ACT.Exp, scale=a_neg[:, g:g + 1]).then_inc(dA_done, 1)

            def rstd(k, mv_done, mv, lnv, lnv_done, r, r_done):
                act.wait_ge(mv_done, k + 1)
                nc.scalar.activation(lnv[:, :], mv[:, :, 1], ACT.Ln, bias=eps_col[:, 0:1]).then_inc(lnv_done, 1)
                act.wait_ge(lnv_done, k + 1)
                nc.scalar.activation(r[:, :], lnv[:, :], ACT.Exp, scale=-0.5).then_inc(r_done, 1)

            def keep_xT(k, par):
                act.wait_ge(xT_made, k + 1)
                nc.scalar.activation(xT[:, HALO + T * par:HALO + T * par + T], w0[:, :], ACT.Copy).then_inc(xT_kept, 1)

            def keep_pre(k, i):
                act.wait_ge(pre_made, 4 * k + i + 1)
                if i < DT:
                    nc.scalar.activation(pre[:, i, :], (w1, w0)[i % 2][:, :], ACT.Identity,
                                         bias=bconv[:, i:i + 1]).then_inc(pre_kept, 1)
                else:
                    nc.scalar.activation(pre[:, i, :], (w1, w0)[i % 2][:, :], ACT.Copy).then_inc(pre_kept, 1)

            def silu_u(k, par):
                act.wait_ge(pre_kept, 4 * k + 4)
                if not (isinstance(k, int) and k < 2):
                    act.wait_ge(y_done, DT * (k - 1))
                nc.scalar.activation(u_res[:, par, :, :], pre[:, :, :], ACT.Silu).then_inc(u_done, 1)

            def keep_b(k, par):
                act.wait_ge(b_made, k + 1)
                if not (isinstance(k, int) and k < 2):
                    act.wait_ge(dbu_done, QUADS * (k - 1))
                nc.scalar.activation(b_rep[:, par, :], w1[:, :], ACT.Copy).then_inc(b_kept, 1)

            def keep_draw(k, i):
                act.wait_ge(draw_made, DT * k + i + 1)
                nc.scalar.activation(a_dt[:, i, :], (w0, w1)[i][:, :], ACT.Abs, bias=bdt[:, i:i + 1]).then_inc(dabs_done, 1)
                nc.scalar.activation(relu_dt[:, i, :], (w0, w1)[i][:, :], ACT.Relu, bias=bdt[:, i:i + 1]).then_inc(dkept, 1)

            def exp_delta(k):
                act.wait_ge(dabs_done, DT * (k + 1))
                nc.scalar.activation(e_dt[:, :, :], a_dt[:, :, :], ACT.Exp, scale=-1.0).then_inc(dexp_done, 1)

            def ln_delta(k):
                nc.scalar.activation(a_dt[:, :, :], e_dt[:, :, :], ACT.Ln, bias=one_col[:, 0:1]).then_inc(dln_done, 1)

            def first_part(k, par):
                act.wait_ge(delta_done, k + 1)
                if not (isinstance(k, int) and k < 1):
                    act.wait_ge(stacked[1 - par], stack_count(k - 1, 1 - par))
                nc.scalar.activation(part[0][:, :, :], delta[:, :, :], ACT.Copy).then_inc(part0_done, 1)

            def second_part(k):
                act.wait_ge(rest_done, k + 1)
                nc.scalar.activation(part[1][:, :, :], rest[:, :, :], ACT.Copy).then_inc(part1_done, 1)

            def keep_x2T(k):
                act.wait_ge(x2T_made, k + 1)
                nc.scalar.activation(x2T[:, :], w1[:, :], ACT.Copy).then_inc(x2T_kept, 1)

            def keep_gate(k, i):
                act.wait_ge(gate_made, HT * k + i + 1)
                nc.scalar.activation(ffn_h[:, i, :], (w0, w1)[i % 2][:, :], ACT.Copy).then_inc(gate_kept, 1)

            def silu_gate(k):
                act.wait_ge(gate_kept, HT * (k + 1))
                nc.scalar.activation(ffn_h[:, :, :], ffn_h[:, :, :], ACT.Silu).then_inc(gate_done, 1)

            def norm1(k):
                rstd(k, mv1_done, mv1, lnv1, lnv1_done, rstd1, rstd1_done)

            def norm2(k):
                rstd(k, mv2_done, mv2, lnv2, lnv2_done, rstd2, rstd2_done)

            act.wait_ge(setup_done, 1)
            norm1(0)
            keep_xT(0, 0)
            norm1(1)
            for i in range(4):
                keep_pre(0, i)
            silu_u(0, 0)
            keep_b(0, 0)
            keep_draw(0, 0)
            keep_draw(0, 1)
            exp_delta(0)
            act.wait_ge(dexp_done, 1)
            ln_delta(0)
            first_part(0, 0)
            second_part(0)
            keep_xT(1, 1)
            exps(0, 0)

            def chunk(k, b, par, has_next, has_after_next, has_previous):
                for s in range(QUADS):
                    if s + 1 < QUADS:
                        exps(k, s + 1)
                    elif has_next:
                        exps(k + 1, 0)
                    if s == 0 and has_next:
                        keep_pre(k + 1, 0)
                    if s == 1:
                        if has_next:
                            keep_pre(k + 1, 1)
                        if has_previous:
                            norm2(k - 1)
                    if s == 2:
                        if has_next:
                            keep_pre(k + 1, 2)
                            keep_pre(k + 1, 3)
                        if has_previous:
                            keep_x2T(k - 1)
                    if s == 3:
                        if has_previous:
                            for i in range(HT):
                                keep_gate(k - 1, i)
                        if has_next:
                            silu_u(k + 1, 1 - par)
                        if has_previous:
                            silu_gate(k - 1)
                    if s == 4 and has_next:
                        keep_b(k + 1, 1 - par)
                        keep_draw(k + 1, 0)
                        keep_draw(k + 1, 1)
                        exp_delta(k + 1)
                        act.wait_ge(dexp_done, k + 2)
                        ln_delta(k + 1)
                    if s == 5 and has_next:
                        first_part(k + 1, 1 - par)
                    if s == 6:
                        if has_next:
                            second_part(k + 1)
                        if has_after_next:
                            norm1(k + 2)
                    if s == 7 and has_after_next:
                        keep_xT(k + 2, par)

            over_chunks(act, chunk)
            norm2(CHUNKS - 1)
            keep_x2T(CHUNKS - 1)
            for i in range(HT):
                keep_gate(CHUNKS - 1, i)
            silu_gate(CHUNKS - 1)

        @block.vector
        def _(dve):
            dve.wait_ge(weights_in, 16 * LOADS)
            for i in range(DT):
                for tap in range(TAPS):
                    nc.vector.tensor_scalar(w_rows[:, CONV + TAPS * i + tap, :], w_in_rows[:, i, :],
                                            conv_w[:, i, tap:tap + 1], None, ALU.mult).then_inc(w_scaled, 1)
            nc.vector.tensor_scalar(w_rows[:, GW:NW, :], w_int[:, :, :], SCALE, None, ALU.mult).then_inc(w_scaled, 1)
            for i in range(6):
                dve.wait_ge(wT_made, i + 1)
                nc.vector.tensor_copy(wT[:, 4 * i:4 * i + 4, :].rearrange("p a b -> p (a b)"), banks[i][:, :])\
                  .then_inc(wT_kept, 1)
            dve.wait_ge(wT_made, 7)
            nc.vector.tensor_copy(wT[:, NW - 1, :], banks[6][:, 0:P])
            nc.vector.tensor_copy(a_exp[:, :], banks[6][:, P:P + GROUPS]).then_inc(wT_kept, 1)
            dve.wait_ge(wT_made, 8)
            nc.vector.tensor_copy(rep[:, :, :].rearrange("p a b -> p (a b)"), banks[7][0:PARTS * 32, :]).then_inc(wT_kept, 1)
            dve.wait_ge(wdelta_made, 1)
            nc.vector.tensor_copy(w_delta[:, :, :].rearrange("p a b -> p (a b)"), banks[0][:, :]).then_inc(wT_kept, 1)
            dve.wait_ge(a_done, 1)
            nc.vector.tensor_scalar(a_neg[:, :], a_exp[:, :], -1.0, None, ALU.mult).then_inc(setup_done, 1)

            def scans(k, par, s):
                slot = s % RING
                dve.wait_ge(dbu_done, QUADS * k + s + 1)
                if par and s == 0:
                    dve.wait_ge(carried, QUADS // 2 * (k - par) + QUADS)
                for c in range(CB):
                    start = carry[:, s, c:c + 1] if par else 0.0
                    dve.wait_ge(dA_done, GROUPS * k + CB * s + c + 1)
                    nc.vector.tensor_tensor_scan(h[:, s % 2, c, :], dA[c][:, :], dbu[:, slot, c, :], start,
                                                 ALU.mult, ALU.add).then_inc(scan_done, 1)

            def times_c(k, par, s):
                dve.wait_ge(scan_done, GROUPS * k + CB * (s + 1))
                if not par:
                    nc.vector.tensor_copy(carry[:, s, :], h[:, s % 2, :, T - 1]).then_inc(carried, 1)
                if s == 0:
                    dve.wait_ge(c_made, k + 1)
                if not (isinstance(k, int) and k == 0 and s < 2):
                    dve.wait_ge(sum_done, QUADS * k + s - 1)
                nc.vector.tensor_tensor(hc[:, s % 2, :, :], h[:, s % 2, :, :],
                                        c_bank[:, :].unsqueeze(1).broadcast_to([P, CB, T]), ALU.mult).then_inc(hc_done, 1)

            def gate_y(k, par, i):
                dve.wait_ge(sum_done, QUADS * k + QPT * (i + 1))
                nc.vector.scalar_tensor_tensor(out=y_skip[:, :], in0=u_res[:, par, i, :], scalar=dskip[:, i:i + 1],
                                               in1=y_bank[:, :], op0=ALU.mult, op1=ALU.add).then_inc(skip_done, 1)
                dve.wait_ge(skip_done, DT * k + i + 1)
                if not (isinstance(k, int) and k < 1):
                    dve.wait_ge(mix_made, k)
                nc.vector.tensor_tensor(y_gated[:, i, :], y_skip[:, :], u_res[:, par, DT + i, :], ALU.mult)\
                  .then_inc(y_done, 1)

            def layer_stats(k, x_of, stats, stats_done, mv, mv_done):
                for a in range(TT):
                    nc.vector.bn_stats(stats[:, a, :], x_of(a)).then_inc(stats_done, 1)
                dve.wait_ge(stats_done, TT * (k + 1))
                nc.vector.tensor_copy(stats_seen[:, :], stats[:, TT - 1, 0:1])
                for a in range(TT):
                    last = nc.vector.bn_aggr(mv[:, a, :], stats[:, a, :])
                last.then_inc(mv_done, 1)

            def layer_norm(k, x_of, mv, r, r_done, y, y_done_sem):
                dve.wait_ge(r_done, k + 1)
                for a in range(TT):
                    last = nc.vector.tensor_scalar(y[:, a, :], x_of(a), mv[:, a, 0:1], r[:, a:a + 1],
                                                   ALU.subtract, ALU.mult)
                last.then_inc(y_done_sem, 1)

            def stats_1(k, par):
                dve.wait_ge(x_loaded[par], x_count(k, par))
                if not (isinstance(k, int) and k < 1):
                    dve.wait_ge(norm1_done, k)
                layer_stats(k, lambda a: x_t[:, par, a, :], stats1, stats1_done, mv1, mv1_done)

            def norm_1(k, par):
                if not (isinstance(k, int) and k < 1):
                    dve.wait_ge(xT_made, k)
                layer_norm(k, lambda a: x_t[:, par, a, :], mv1, rstd1, rstd1_done, xn, norm1_done)

            def add_mix(k, par):
                dve.wait_ge(mix_made, k + 1)
                dve.wait_ge(x_reloaded[par], x_count(k, par))
                nc.vector.tensor_tensor(x2[:, :, :], x_again[:, par, :, :],
                                        w0[:, :].rearrange("p (a b) -> p a b", a=TT), ALU.add).then_inc(x2_done, 1)

            def stats_2(k):
                dve.wait_ge(x2_done, k + 1)
                layer_stats(k, lambda a: x2[:, a, :], stats2, stats2_done, mv2, mv2_done)

            def norm_2(k):
                layer_norm(k, lambda a: x2[:, a, :], mv2, rstd2, rstd2_done, x2n, norm2_done)

            def series_factor(k):
                dve.wait_ge(dexp_done, k + 1)
                nc.vector.tensor_scalar(s_dt[:, :, :], e_dt[:, :, :], 1.0 / 3.0, -0.5, ALU.mult, ALU.add)\
                  .then_inc(dfactor_done, 1)

            def softplus(k):
                dve.wait_ge(dsquare_done, k + 1)
                nc.vector.scalar_tensor_tensor(out=s_dt[:, :, :], in0=s_dt[:, :, :], scalar=1.0, in1=e_dt[:, :, :],
                                               op0=ALU.add, op1=ALU.mult).then_inc(dseries_done, 1)
                dve.wait_ge(dseries_done, k + 1)
                dve.wait_ge(dln_done, k + 1)
                nc.vector.tensor_tensor(s_dt[:, :, :], s_dt[:, :, :], a_dt[:, :, :], ALU.min).then_inc(dlog_done, 1)

            def times_up(k, i):
                dve.wait_ge(up_made, HT * k + i + 1)
                if i == 0:
                    dve.wait_ge(gate_done, k + 1)
                nc.vector.tensor_tensor(ffn_h[:, i, :], ffn_h[:, i, :], (w0, w1)[i % 2][:, :], ALU.mult)\
                  .then_inc(ffn_h_done, 1)

            def finish(k, par):
                dve.wait_ge(down_made, k + 1)
                if not (isinstance(k, int) and k < 2):
                    dve.wait_ge(stored[par], x_count(k - 2, par))
                nc.vector.tensor_tensor(fin[:, par, :, :], x2[:, :, :],
                                        w1[:, :].rearrange("p (a b) -> p a b", a=TT), ALU.add).then_inc(fin_done, 1)

            stats_1(0, 0)
            norm_1(0, 0)
            stats_1(1, 1)
            series_factor(0)
            softplus(0)
            norm_1(1, 1)

            def chunk(k, b, par, has_next, has_after_next, has_previous):
                for s in range(QUADS):
                    scans(k, par, s)
                    if s == 0 and has_previous:
                        gate_y(k - 1, 1 - par, 1)
                    if s == 4:
                        gate_y(k, par, 0)
                    times_c(k, par, s)
                    if s == 1 and has_previous:
                        add_mix(k - 1, 1 - par)
                        stats_2(k - 1)
                    if s == 2 and has_previous:
                        norm_2(k - 1)
                    if s == 3 and has_after_next:
                        stats_1(k + 2, par)
                    if s == 4 and has_next:
                        series_factor(k + 1)
                    if s == 5 and has_next:
                        softplus(k + 1)
                    if s == 6 and has_previous:
                        for i in range(HT):
                            times_up(k - 1, i)
                    if s == 7:
                        if has_after_next:
                            norm_1(k + 2, par)
                        if has_previous:
                            finish(k - 1, 1 - par)

            over_chunks(dve, chunk)
            last = CHUNKS - 1
            gate_y(last, 1, 1)
            add_mix(last, 1)
            stats_2(last)
            norm_2(last)
            for i in range(HT):
                times_up(last, i)
            finish(last, 1)

        @block.tensor
        def _(pe):
            pe.wait_ge(weights_in, 16 * LOADS)
            pe.wait_ge(consts_set, 6)
            pe.wait_ge(w_scaled, DT * TAPS + 1)
            for i in range(6):
                for j in range(4):
                    last = nc.tensor.transpose(banks[i][:, P * j:P * j + P], w_rows[:, 4 * i + j, :], ident[:, :])
                last.then_inc(wT_made, 1)
            nc.tensor.transpose(banks[6][:, 0:P], w_rows[:, NW - 1, :], ident[:, :])
            nc.tensor.transpose(banks[6][:, P:P + GROUPS], alog_rows[:, :], ident[0:GROUPS, 0:GROUPS]).then_inc(wT_made, 1)
            for q in range(QPT):
                last = nc.tensor.transpose(banks[7][0:PARTS * 32, P * q:P * q + P],
                                           sel[:, q, :, :].rearrange("p a b -> p (a b)"), ident[:, :])
            last.then_inc(wT_made, 1)
            pe.wait_ge(wT_kept, 1)
            for i in range(DT):
                last = nc.tensor.matmul(banks[0][:, DI * i:DI * i + DI], wx_dt[:, P * i:P * i + P], wdt_T[:, :],
                                        start=True, stop=True)
            last.then_inc(wdelta_made, 1)
            pe.wait_ge(wT_kept, 9)

            def bank_free(sem_, n):
                pe.wait_ge(sem_, n)

            def transpose_x(k):
                pe.wait_ge(norm1_done, k + 1)
                for a in range(TT):
                    last = nc.tensor.transpose(w0[:, P * a:P * a + P], xn[:, a, :], ident[:, :])
                last.then_inc(xT_made, 1)

            def project_pre(k, par, i):
                if i == 0:
                    pe.wait_ge(xT_kept, k + 1)
                bank = (w1, w0)[i % 2]
                at = T * par
                if i < DT:
                    for tap in range(TAPS):
                        last = nc.tensor.matmul(bank[:, :], wT[:, CONV + TAPS * i + tap, :], xT[:, at + tap:at + tap + T],
                                                start=(tap == 0), stop=(tap == TAPS - 1))
                else:
                    last = nc.tensor.matmul(bank[:, :], wT[:, RES + i - DT, :], xT[:, at + HALO:at + HALO + T],
                                            start=True, stop=True)
                last.then_inc(pre_made, 1)

            def project_b(k, par):
                pe.wait_ge(u_done, k + 1)
                for i in range(DT):
                    last = nc.tensor.matmul(w1[:, :], wT[:, BW + i, :], u_res[:, par, i, :],
                                            start=(i == 0), stop=(i == DT - 1))
                last.then_inc(b_made, 1)

            def project_delta(k, par, i):
                for j in range(DT):
                    last = nc.tensor.matmul((w0, w1)[i][:, :], w_delta[:, j, P * i:P * i + P], u_res[:, par, j, :],
                                            start=(j == 0), stop=(j == DT - 1))
                last.then_inc(draw_made, 1)

            def project_c(k, par):
                if not (isinstance(k, int) and k == 0):
                    pe.wait_ge(hc_done, QUADS * k)
                for i in range(DT):
                    last = nc.tensor.matmul(c_bank[:, :], wT[:, CW + i, :], u_res[:, par, i, :],
                                            start=(i == 0), stop=(i == DT - 1))
                last.then_inc(c_made, 1)

            def spread_delta(k, par, s):
                tile, sub = s // QPT, s % QPT
                if s == 0:
                    pe.wait_ge(stacked[par], stack_count(k, par))
                for c in range(CB):
                    if not (isinstance(k, int) and k == 0 and s == 0):
                        pe.wait_ge(scan_done, GROUPS * k + CB * (s - 1) + c + 1)
                    nc.tensor.matmul(dA[c][:, :], rep[:, sub, :], stack[:, par, c, tile, :],
                                     start=True, stop=True).then_inc(delta_spread, 1)

            def sum_states(k, s):
                sub = s % QPT
                pe.wait_ge(hc_done, QUADS * k + s + 1)
                if sub == 0 and not (isinstance(k, int) and k == 0 and s == 0):
                    pe.wait_ge(skip_done, DT * k + s // QPT)
                for c in range(CB):
                    last = nc.tensor.matmul(y_bank[32 * c:32 * c + 32, :], sel[:, sub, 0, :], hc[:, s % 2, c, :],
                                            start=(sub == 0), stop=(sub == QPT - 1))
                last.then_inc(sum_done, 1)

            def project_mix(k):
                pe.wait_ge(y_done, DT * (k + 1))
                for a in range(TT):
                    for i in range(DT):
                        last = nc.tensor.matmul(w0[:, P * a:P * a + P], y_gated[:, i, P * a:P * a + P], wT[:, OW + i, :],
                                                start=(i == 0), stop=(i == DT - 1))
                last.then_inc(mix_made, 1)

            def transpose_x2(k):
                pe.wait_ge(norm2_done, k + 1)
                for a in range(TT):
                    last = nc.tensor.transpose(w1[:, P * a:P * a + P], x2n[:, a, :], ident[:, :])
                last.then_inc(x2T_made, 1)

            def project_gate(k, i):
                if i == 0:
                    pe.wait_ge(x2T_kept, k + 1)
                nc.tensor.matmul((w0, w1)[i % 2][:, :], wT[:, GW + i, :], x2T[:, :], start=True, stop=True)\
                  .then_inc(gate_made, 1)

            def project_up(k, i):
                nc.tensor.matmul((w0, w1)[i % 2][:, :], wT[:, UW + i, :], x2T[:, :], start=True, stop=True)\
                  .then_inc(up_made, 1)

            def project_down(k):
                pe.wait_ge(ffn_h_done, HT * (k + 1))
                for a in range(TT):
                    for i in range(HT):
                        last = nc.tensor.matmul(w1[:, P * a:P * a + P], ffn_h[:, i, P * a:P * a + P], wT[:, DW + i, :],
                                                start=(i == 0), stop=(i == HT - 1))
                last.then_inc(down_made, 1)

            transpose_x(0)
            project_pre(0, 0, 0)
            bank_free(xT_kept, 1)
            project_pre(0, 0, 1)
            bank_free(pre_kept, 1)
            project_pre(0, 0, 2)
            bank_free(pre_kept, 2)
            project_pre(0, 0, 3)
            bank_free(pre_kept, 4)
            project_b(0, 0)
            project_delta(0, 0, 0)
            bank_free(b_kept, 1)
            project_delta(0, 0, 1)
            spread_delta(0, 0, 0)
            bank_free(dkept, DT)
            transpose_x(1)

            def chunk(k, b, par, has_next, has_after_next, has_previous):
                nxt = 1 - par
                for s in range(QUADS):
                    if s == 0:
                        project_c(k, par)
                        if has_previous:
                            sum_states(k - 1, QUADS - 1)
                    else:
                        sum_states(k, s - 1)
                    if s + 1 < QUADS:
                        spread_delta(k, par, s + 1)
                    elif has_next:
                        spread_delta(k + 1, nxt, 0)
                    if s == 0:
                        if has_previous:
                            if has_next:
                                bank_free(xT_kept, k + 2)
                            project_mix(k - 1)
                        if has_next:
                            if has_previous and not (isinstance(k, int) and k == 1):
                                bank_free(fin_done, k - 1)
                            project_pre(k + 1, nxt, 0)
                    if s == 1 and has_next:
                        bank_free(x2_done, k) if has_previous else bank_free(xT_kept, k + 2)
                        project_pre(k + 1, nxt, 1)
                    if s == 2:
                        if has_next:
                            bank_free(pre_kept, 4 * (k + 1) + 1)
                            project_pre(k + 1, nxt, 2)
                            bank_free(pre_kept, 4 * (k + 1) + 2)
                            project_pre(k + 1, nxt, 3)
                            bank_free(pre_kept, 4 * (k + 1) + 3)
                        else:
                            bank_free(fin_done, k - 1)
                        if has_previous:
                            transpose_x2(k - 1)
                    if s == 3 and has_previous:
                        if has_next:
                            bank_free(pre_kept, 4 * (k + 1) + 4)
                        else:
                            bank_free(x2_done, k)
                        project_gate(k - 1, 0)
                        project_gate(k - 1, 1)
                        bank_free(gate_kept, HT * (k - 1) + 1)
                        project_gate(k - 1, 2)
                    if s == 4:
                        if has_next:
                            if has_previous:
                                bank_free(gate_kept, HT * (k - 1) + 2)
                            else:
                                bank_free(pre_kept, 4 * (k + 1) + 4)
                            project_b(k + 1, nxt)
                            if has_previous:
                                bank_free(gate_kept, HT * k)
                            project_delta(k + 1, nxt, 0)
                            bank_free(b_kept, k + 2)
                            project_delta(k + 1, nxt, 1)
                    if s == 6 and has_previous:
                        if has_next:
                            bank_free(dkept, DT * (k + 2))
                        else:
                            bank_free(gate_kept, HT * k)
                        project_up(k - 1, 0)
                        project_up(k - 1, 1)
                        bank_free(ffn_h_done, HT * (k - 1) + 1)
                        project_up(k - 1, 2)
                    if s == 7:
                        if has_previous:
                            project_down(k - 1)
                        if has_after_next:
                            if not has_previous:
                                bank_free(dkept, DT * (k + 2))
                            transpose_x(k + 2)

            over_chunks(pe, chunk)
            last_k = CHUNKS - 1
            sum_states(last_k, QUADS - 1)
            project_mix(last_k)
            bank_free(fin_done, last_k)
            transpose_x2(last_k)
            bank_free(x2_done, CHUNKS)
            project_gate(last_k, 0)
            project_gate(last_k, 1)
            bank_free(gate_kept, HT * last_k + 1)
            project_gate(last_k, 2)
            bank_free(gate_kept, HT * CHUNKS)
            project_up(last_k, 0)
            project_up(last_k, 1)
            bank_free(ffn_h_done, HT * last_k + 1)
            project_up(last_k, 2)
            project_down(last_k)


_INS = ['L0_attn_x', 'L0_attn_W_in', 'L0_attn_W_conv', 'L0_attn_b_conv', 'L0_attn_W_xproj', 'L0_attn_W_dt',
        'L0_attn_b_dt', 'L0_attn_A_log', 'L0_attn_D', 'L0_attn_W_out', 'L0_ffn_w_gate', 'L0_ffn_w_up', 'L0_ffn_w_down']
_OUT_SHAPE = (8, 1024, 128)


def kernel(**inputs):
    import numpy as _np
    import concourse.bacc as _bacc
    from concourse import mybir as _mybir
    from concourse.bass_utils import run_bass_kernel_spmd as _run

    nc = _bacc.Bacc("TRN2", target_bir_lowering=False, num_devices=1)
    arrays, args = {}, []
    for name in _INS:
        a = _np.ascontiguousarray(inputs[name])
        arrays[f"in_{name}"] = a
        args.append(nc.dram_tensor(f"in_{name}", a.shape, _mybir.dt.from_np(a.dtype), kind="ExternalInput").ap())
    args.append(nc.dram_tensor("out_0", _OUT_SHAPE, _mybir.dt.float32, kind="ExternalOutput").ap())
    mamba_block_and_gated_ffn(nc, *args)
    r = _run(nc, [arrays], core_ids=[0])
    return r.results[0]["out_0"]
```

```python
import concourse.bass as bass
from concourse import mybir
from contextlib import ExitStack


def mamba_block_and_gated_ffn(
    nc: bass.Bass,
    x_in: bass.AP,
    W_in: bass.AP,
    W_conv: bass.AP,
    b_conv: bass.AP,
    W_xproj: bass.AP,
    W_dt: bass.AP,
    b_dt: bass.AP,
    A_log: bass.AP,
    D_skip: bass.AP,
    W_out: bass.AP,
    w_gate: bass.AP,
    w_up: bass.AP,
    w_down: bass.AP,
    out: bass.AP,
):
    fp32 = mybir.dt.float32
    bf16 = mybir.dt.bfloat16
    int32 = mybir.dt.int32
    ALU = mybir.AluOpType
    ACT = mybir.ActivationFunctionType

    BATCH, SEQ, DIM = x_in.shape
    DI = W_dt.shape[0]
    R = W_dt.shape[1]
    NS = A_log.shape[1]
    HID = w_gate.shape[0]
    TAPS = W_conv.shape[2]
    SCALE = 1.0 / 127.0
    EPS = 1e-5
    LN_SHIFT = 2.0 ** -22
    P = 128
    T = 512
    TT = T // P
    CPB = SEQ // T
    CHUNKS = BATCH * CPB
    DT = DI // P
    HT = HID // P
    GD = P // NS
    CB = 4
    QPT = P // 32 * 4 // CB
    QUADS = DT * QPT
    GROUPS = QUADS * CB
    PARTS = 3
    HALO = TAPS - 1
    RING = 4
    assert CPB == 2 and DIM == P and GD == 8 and QUADS == 8

    x_v = x_in.rearrange("b (c a p) d -> (b c) p a d", c=CPB, p=P)
    out_v = out.rearrange("b (c a p) d -> (b c) p a d", c=CPB, p=P)

    ctx = ExitStack()
    with ctx:
        def sb(name, shape, dt=fp32):
            return ctx.enter_context(nc.sbuf_tensor(name, shape, dt))

        def sem(name):
            return ctx.enter_context(nc.semaphore(name))

        CONV, RES, BW, CW, OW, GW, UW, DW = 0, 8, 10, 12, 14, 16, 19, 22
        NW = 25
        dbu = sb("dbu", [P, RING, CB, T])
        dbu_flat = dbu[:, :, :, :].rearrange("p r c t -> p (r c t)")
        w_rows = dbu_flat[:, 0:NW * P].rearrange("p (w m) -> p w m", m=P)
        w_int = dbu_flat[:, NW * P:(2 * NW - GW) * P].bitcast(int32).rearrange("p (w m) -> p w m", m=P)
        w_in_rows = sb("w_in_rows", [P, DT, P])
        conv_w = sb("conv_w", [P, DT, TAPS])
        alog_rows = sb("alog_rows", [GROUPS, P])
        wx_dt = sb("wx_dt", [R, DI])
        wdt_T = sb("wdt_T", [R, DI])
        bconv = sb("bconv", [P, DT])
        bdt = sb("bdt", [P, DT])
        dskip = sb("dskip", [P, DT])
        wT = sb("wT", [P, NW, P])
        w_delta = sb("w_delta", [P, DT, DI])
        a_exp = sb("a_exp", [P, GROUPS])
        a_neg = sb("a_neg", [P, GROUPS])
        ident = sb("ident", [P, P])
        sel = sb("sel", [P, QPT, PARTS, 32])
        rep = sb("rep", [PARTS * 32, QPT, P], bf16)
        eps_col = sb("eps_col", [P, 1])
        one_col = sb("one_col", [P, 1])
        zero_col = sb("zero_col", [P, 1])

        x_t = sb("x_t", [P, 2, TT, P])
        x_again = sb("x_again", [P, 2, TT, P])
        stats_seen = sb("stats_seen", [P, 1])
        stats1 = sb("stats1", [P, TT, 6])
        mv1 = sb("mv1", [P, TT, 2])
        lnv1 = sb("lnv1", [P, TT])
        rstd1 = sb("rstd1", [P, TT])
        xn = sb("xn", [P, TT, P])
        xT = sb("xT", [P, HALO + 1 + CPB * T])
        pre = sb("pre", [P, 2 * DT, T])
        u_res = sb("u_res", [P, 2, 2 * DT, T])
        b_rep = sb("b_rep", [P, 2, T])
        a_dt = sb("a_dt", [P, DT, T])
        relu_dt = sb("relu_dt", [P, DT, T])
        e_dt = sb("e_dt", [P, DT, T])
        s_dt = sb("s_dt", [P, DT, T])
        delta = sb("delta", [P, DT, T])
        rest = sb("rest", [P, DT, T])
        part = [sb(f"part{j}", [P, DT, T], bf16) for j in range(PARTS)]
        stack = sb("stack", [PARTS * 32, 2, CB, DT, T], bf16)
        du = sb("du", [P, 2, DT, T])
        h = sb("h", [P, 2, CB, T])
        carry = sb("carry", [P, QUADS, CB])
        hc = sb("hc", [P, 2, CB, T])
        y_skip = sb("y_skip", [P, T])
        y_gated = sb("y_gated", [P, DT, T])
        x2 = sb("x2", [P, TT, P])
        stats2 = sb("stats2", [P, TT, 6])
        mv2 = sb("mv2", [P, TT, 2])
        lnv2 = sb("lnv2", [P, TT])
        rstd2 = sb("rstd2", [P, TT])
        x2n = sb("x2n", [P, TT, P])
        x2T = sb("x2T", [P, T])
        ffn_h = sb("ffn_h", [P, HT, T])
        fin = sb("fin", [P, 2, TT, P])

        banks = [ctx.enter_context(nc.psum_tensor(f"bank{i}", [P, T], fp32)) for i in range(8)]
        dA = banks[0:4]
        c_bank, y_bank, w0, w1 = banks[4:8]

        weights_in = sem("weights_in")
        consts_set = sem("consts_set")
        sel_step = sem("sel_step")
        w_scaled = sem("w_scaled")
        wT_made = sem("wT_made")
        wT_kept = sem("wT_kept")
        wdelta_made = sem("wdelta_made")
        a_done = sem("a_done")
        setup_done = sem("setup_done")

        x_loaded = [sem(f"x_loaded{i}") for i in range(2)]
        x_reloaded = [sem(f"x_reloaded{i}") for i in range(2)]
        stats1_done = sem("stats1_done")
        mv1_done = sem("mv1_done")
        lnv1_done = sem("lnv1_done")
        rstd1_done = sem("rstd1_done")
        norm1_done = sem("norm1_done")
        xT_made = sem("xT_made")
        xT_kept = sem("xT_kept")
        pre_made = sem("pre_made")
        pre_kept = sem("pre_kept")
        u_done = sem("u_done")
        b_made = sem("b_made")
        b_kept = sem("b_kept")
        draw_made = sem("draw_made")
        dexp_done = sem("dexp_done")
        dabs_done = sem("dabs_done")
        dkept = sem("dkept")
        dfactor_done = sem("dfactor_done")
        dsquare_done = sem("dsquare_done")
        dseries_done = sem("dseries_done")
        dlog_done = sem("dlog_done")
        dln_done = sem("dln_done")
        delta_done = sem("delta_done")
        du_done = sem("du_done")
        part0_done = sem("part0_done")
        rest_done = sem("rest_done")
        part1_done = sem("part1_done")
        part2_done = sem("part2_done")
        stacked = [sem(f"stacked{i}") for i in range(2)]
        du_spread = [sem(f"du_spread{i}") for i in range(RING)]
        dbu_done = sem("dbu_done")
        delta_spread = sem("delta_spread")
        dA_done = sem("dA_done")
        c_made = sem("c_made")
        scan_done = sem("scan_done")
        carried = sem("carried")
        hc_done = sem("hc_done")
        sum_done = sem("sum_done")
        skip_done = sem("skip_done")
        y_done = sem("y_done")
        mix_made = sem("mix_made")
        x2_done = sem("x2_done")
        stats2_done = sem("stats2_done")
        mv2_done = sem("mv2_done")
        lnv2_done = sem("lnv2_done")
        rstd2_done = sem("rstd2_done")
        norm2_done = sem("norm2_done")
        x2T_made = sem("x2T_made")
        x2T_kept = sem("x2T_kept")
        gate_made = sem("gate_made")
        gate_kept = sem("gate_kept")
        gate_done = sem("gate_done")
        up_made = sem("up_made")
        ffn_h_done = sem("ffn_h_done")
        down_made = sem("down_made")
        fin_done = sem("fin_done")
        stored = [sem(f"stored{i}") for i in range(2)]

        block = ctx.enter_context(nc.Block())
        LOADS = 15

        def over_chunks(eng, chunk):
            def batch(b, first, last):
                for c in range(CPB):
                    chunk(b * CPB + c, c, not (last and c == CPB - 1), not last,
                          not (first and c == 0), not first)
            batch(0, True, False)
            with eng.Fori(1, BATCH - 1) as b:
                batch(b, False, False)
            batch(BATCH - 1, False, True)

        def stack_count(k, par):
            return 8 * PARTS * CB * (k - par + 2)

        def x_count(k, par):
            return 8 * (k - par + 2)

        @block.sync
        def _(sp):
            def load_x(k, par):
                sp.dma_start(x_t[:, par, :, :], x_v[k, :, :, :]).then_inc(x_loaded[par], 16)

            load_x(0, 0)
            sp.dma_start(w_in_rows[:, :, :], W_in[0:DI, :].rearrange("(t p) m -> p t m", p=P)).then_inc(weights_in, 16)
            sp.dma_start(w_rows[:, RES:RES + DT, :], W_in[DI:2 * DI, :].rearrange("(t p) m -> p t m", p=P)).then_inc(weights_in, 16)
            sp.dma_start(conv_w[:, :, :], W_conv.rearrange("(t p) o k -> p t (o k)", p=P)).then_inc(weights_in, 16)
            sp.dma_start(alog_rows[:, :], A_log.rearrange("(g l) n -> g (l n)", g=GROUPS)).then_inc(weights_in, 16)
            sp.dma_start(wx_dt[:, :], W_xproj[0:R, :]).then_inc(weights_in, 16)
            sp.dma_start(wdt_T[:, :], W_dt.rearrange("d r -> r d"), allow_slow_non_contiguous=True).then_inc(weights_in, 16)
            for col, vec in ((bconv, b_conv), (bdt, b_dt), (dskip, D_skip)):
                sp.dma_start(col[:, :], vec.rearrange("(t p) -> p t", p=P), allow_slow_non_contiguous=True).then_inc(weights_in, 16)
            for at, row in ((BW, R), (CW, R + NS)):
                rows = W_xproj[row:row + NS, :].rearrange("n (t m) -> n t m", t=DT)
                sp.dma_start(w_rows[:, at:at + DT, :], rows.unsqueeze(0).broadcast_to([GD, NS, DT, P])).then_inc(weights_in, 16)
            sp.dma_start(w_rows[:, OW:OW + DT, :], W_out.rearrange("m (t p) -> m t p", p=P)).then_inc(weights_in, 16)
            sp.dma_start(w_int[:, 0:HT, :], w_gate.rearrange("(t p) m -> p t m", p=P)).then_inc(weights_in, 16)
            sp.dma_start(w_int[:, HT:2 * HT, :], w_up.rearrange("(t p) m -> p t m", p=P)).then_inc(weights_in, 16)
            sp.dma_start(w_int[:, 2 * HT:3 * HT, :], w_down.rearrange("m (t p) -> m t p", p=P)).then_inc(weights_in, 16)

            load_x(1, 1)

            def reload_x(k, par):
                sp.dma_start(x_again[:, par, :, :], x_v[k, :, :, :]).then_inc(x_reloaded[par], 16)

            def spread_du(par, q):
                tile, sub, slot = q // QPT, q % QPT, q % RING
                for c in range(CB):
                    row = 32 * c + GD * sub
                    sp.dma_start(dbu[:, slot, c, :],
                                 du[row:row + GD, par, tile, :].unsqueeze(1).broadcast_to([GD, NS, T]))\
                      .then_inc(du_spread[slot], 16)

            def stack_delta(par, j):
                for c in range(CB):
                    sp.dma_start(stack[32 * j:32 * j + 32, par, c, :, :],
                                 part[j][32 * c:32 * c + 32, :, :]).then_inc(stacked[par], 16)

            def store(k, par):
                sp.wait_ge(fin_done, k + 1)
                sp.dma_start(out_v[k, :, :, :], fin[:, par, :, :]).then_inc(stored[par], 16)

            sp.wait_ge(du_done, 1)
            spread_du(0, 0)
            for j in range(PARTS):
                sp.wait_ge((part0_done, part1_done, part2_done)[j], 1)
                stack_delta(0, j)
            spread_du(0, 1)
            spread_du(0, 2)
            spread_du(0, 3)

            def chunk(k, par, has_next, has_after_next, has_previous, has_before_previous):
                nxt = 1 - par
                if has_after_next:
                    sp.wait_ge(norm1_done, k + 1)
                    load_x(k + 2, par)
                if has_previous and not (isinstance(k, int) and k == 1):
                    sp.wait_ge(x2_done, k - 1)
                reload_x(k, par)
                for s in range(RING, QUADS):
                    sp.wait_ge(scan_done, GROUPS * k + CB * (s - RING + 1))
                    spread_du(par, s)
                    if s == RING and has_before_previous:
                        store(k - 2, par)
                if has_next:
                    sp.wait_ge(weights_in, 16 * LOADS)
                    sp.wait_ge(du_done, k + 2)
                    sp.wait_ge(scan_done, GROUPS * k + CB * (RING + 1))
                    spread_du(nxt, 0)
                    sp.wait_ge(part0_done, k + 2)
                    stack_delta(nxt, 0)
                    sp.wait_ge(part1_done, k + 2)
                    stack_delta(nxt, 1)
                    sp.wait_ge(part2_done, k + 2)
                    stack_delta(nxt, 2)
                    for s in range(1, RING):
                        sp.wait_ge(scan_done, GROUPS * k + CB * (s + RING + 1))
                        spread_du(nxt, s)

            over_chunks(sp, chunk)
            store(CHUNKS - 2, 0)
            store(CHUNKS - 1, 1)
            for par in range(2):
                sp.wait_ge(stored[par], 16 * CHUNKS // 2)

        @block.gpsimd
        def _(pool):
            nc.gpsimd.memset(ident[:, :], 0.0).then_inc(sel_step, 1)
            nc.gpsimd.memset(sel[:, :, :, :], 1.0).then_inc(sel_step, 1)
            nc.gpsimd.memset(eps_col[:, :], EPS).then_inc(consts_set, 1)
            nc.gpsimd.memset(one_col[:, :], 1.0 + LN_SHIFT).then_inc(consts_set, 1)
            nc.gpsimd.memset(zero_col[:, :], 0.0).then_inc(consts_set, 1)
            nc.gpsimd.memset(xT[:, 0:HALO], 0.0).then_inc(consts_set, 1)
            pool.wait_ge(sel_step, 2)
            nc.gpsimd.affine_select(out=ident[:, :], in_=ident[:, :], compare_op=ALU.not_equal, fill=1.0,
                                    base=0, pattern=[[-1, P]], channel_multiplier=1).then_inc(consts_set, 1)
            nc.gpsimd.affine_select(out=sel[:, :, :, :], in_=sel[:, :, :, :], compare_op=ALU.is_ge, fill=0.0,
                                    base=0, pattern=[[P, QPT], [0, PARTS], [-NS, 32]], channel_multiplier=1)\
              .then_inc(sel_step, 1)
            pool.wait_ge(sel_step, 3)
            nc.gpsimd.affine_select(out=sel[:, :, :, :], in_=sel[:, :, :, :], compare_op=ALU.is_ge, fill=0.0,
                                    base=NS - 1, pattern=[[-P, QPT], [0, PARTS], [NS, 32]], channel_multiplier=-1)\
              .then_inc(consts_set, 1)

            def times_b(k, par, s, turn):
                slot = s % RING
                pool.wait_ge(du_spread[slot], 16 * CB * turn)
                if s == 0:
                    pool.wait_ge(b_kept, k + 1)
                nc.gpsimd.tensor_tensor(dbu[:, slot, :, :], dbu[:, slot, :, :],
                                        b_rep[:, par, :].unsqueeze(1).broadcast_to([P, CB, T]), ALU.mult)\
                  .then_inc(dbu_done, 1)

            def times_e(k):
                pool.wait_ge(dfactor_done, k + 1)
                nc.gpsimd.tensor_tensor(s_dt[:, :, :], s_dt[:, :, :], e_dt[:, :, :], ALU.mult).then_inc(dsquare_done, 1)

            def add_relu(k):
                pool.wait_ge(dlog_done, k + 1)
                if not (isinstance(k, int) and k < 1):
                    pool.wait_ge(part0_done, k)
                nc.gpsimd.tensor_tensor(delta[:, :, :], relu_dt[:, :, :], s_dt[:, :, :], ALU.add).then_inc(delta_done, 1)

            def times_u(k, par):
                pool.wait_ge(delta_done, k + 1)
                if not (isinstance(k, int) and k < 2):
                    pool.wait_ge(dbu_done, QUADS * (k - 1))
                nc.gpsimd.tensor_tensor(du[:, par, :, :], delta[:, :, :], u_res[:, par, 0:DT, :], ALU.mult)\
                  .then_inc(du_done, 1)

            def first_rest(k):
                pool.wait_ge(part0_done, k + 1)
                nc.gpsimd.tensor_tensor(rest[:, :, :], delta[:, :, :], part[0][:, :, :], ALU.subtract)\
                  .then_inc(rest_done, 1)

            def last_part(k, par):
                pool.wait_ge(part1_done, k + 1)
                if not (isinstance(k, int) and k < 1):
                    pool.wait_ge(stacked[1 - par], stack_count(k - 1, 1 - par))
                nc.gpsimd.tensor_tensor(part[2][:, :, :], rest[:, :, :], part[1][:, :, :], ALU.subtract)\
                  .then_inc(part2_done, 1)

            times_e(0)
            add_relu(0)
            times_u(0, 0)
            first_rest(0)
            last_part(0, 0)
            times_b(0, 0, 0, 1)
            times_b(0, 0, 1, 1)

            def chunk(k, par, has_next, has_after_next, has_previous, has_before_previous):
                for s in range(QUADS):
                    if has_next and s == 2:
                        times_e(k + 1)
                    if has_next and s == 3:
                        add_relu(k + 1)
                    if has_next and s == 4:
                        times_u(k + 1, 1 - par)
                        first_rest(k + 1)
                    if has_next and s == 5:
                        last_part(k + 1, 1 - par)
                    if s + 2 < QUADS:
                        times_b(k, par, s + 2, 2 * k + (s + 2) // RING + 1)
                    elif has_next:
                        times_b(k + 1, 1 - par, s + 2 - QUADS, 2 * k + 3)

            over_chunks(pool, chunk)

        @block.scalar
        def _(act):
            def exps(k, s):
                tile, sub = s // QPT, s % QPT
                for c in range(CB):
                    g = tile * QPT * CB + QPT * c + sub
                    act.wait_ge(delta_spread, GROUPS * k + CB * s + c + 1)
                    nc.scalar.activation(dA[c][:, :], dA[c][:, :], ACT.Exp, scale=a_neg[:, g:g + 1]).then_inc(dA_done, 1)

            def rstd(k, mv_done, mv, lnv, lnv_done, r, r_done):
                act.wait_ge(mv_done, k + 1)
                nc.scalar.activation(lnv[:, :], mv[:, :, 1], ACT.Ln, bias=eps_col[:, 0:1]).then_inc(lnv_done, 1)
                act.wait_ge(lnv_done, k + 1)
                nc.scalar.activation(r[:, :], lnv[:, :], ACT.Exp, scale=-0.5).then_inc(r_done, 1)

            def keep_xT(k, par):
                act.wait_ge(xT_made, k + 1)
                nc.scalar.activation(xT[:, HALO + T * par:HALO + T * par + T], w0[:, :], ACT.Copy).then_inc(xT_kept, 1)

            def keep_pre(k, i):
                act.wait_ge(pre_made, 4 * k + i + 1)
                if i < DT:
                    nc.scalar.activation(pre[:, i, :], (w1, w0, w1, w1)[i][:, :], ACT.Identity,
                                         bias=bconv[:, i:i + 1]).then_inc(pre_kept, 1)
                else:
                    nc.scalar.activation(pre[:, i, :], (w1, w0, w1, w1)[i][:, :], ACT.Copy).then_inc(pre_kept, 1)

            def silu_u(k, par):
                act.wait_ge(pre_kept, 4 * k + 4)
                if not (isinstance(k, int) and k < 2):
                    act.wait_ge(y_done, DT * (k - 1))
                nc.scalar.activation(u_res[:, par, :, :], pre[:, :, :], ACT.Silu).then_inc(u_done, 1)

            def keep_b(k, par):
                act.wait_ge(b_made, k + 1)
                if not (isinstance(k, int) and k < 2):
                    act.wait_ge(dbu_done, QUADS * (k - 1))
                nc.scalar.activation(b_rep[:, par, :], w1[:, :], ACT.Copy).then_inc(b_kept, 1)

            def keep_draw(k, i):
                act.wait_ge(draw_made, DT * k + i + 1)
                nc.scalar.activation(a_dt[:, i, :], (w0, w1)[i][:, :], ACT.Abs, bias=bdt[:, i:i + 1]).then_inc(dabs_done, 1)
                nc.scalar.activation(relu_dt[:, i, :], (w0, w1)[i][:, :], ACT.Relu, bias=bdt[:, i:i + 1]).then_inc(dkept, 1)

            def exp_delta(k):
                act.wait_ge(dabs_done, DT * (k + 1))
                nc.scalar.activation(e_dt[:, :, :], a_dt[:, :, :], ACT.Exp, scale=-1.0).then_inc(dexp_done, 1)

            def ln_delta(k):
                act.wait_ge(dexp_done, k + 1)
                nc.scalar.activation(a_dt[:, :, :], e_dt[:, :, :], ACT.Ln, bias=one_col[:, 0:1]).then_inc(dln_done, 1)

            def first_part(k, par):
                act.wait_ge(delta_done, k + 1)
                if not (isinstance(k, int) and k < 1):
                    act.wait_ge(stacked[1 - par], stack_count(k - 1, 1 - par))
                nc.scalar.activation(part[0][:, :, :], delta[:, :, :], ACT.Copy).then_inc(part0_done, 1)

            def second_part(k):
                act.wait_ge(rest_done, k + 1)
                nc.scalar.activation(part[1][:, :, :], rest[:, :, :], ACT.Copy).then_inc(part1_done, 1)

            def keep_x2T(k):
                act.wait_ge(x2T_made, k + 1)
                nc.scalar.activation(x2T[:, :], w1[:, :], ACT.Copy).then_inc(x2T_kept, 1)

            def keep_gate(k, i):
                act.wait_ge(gate_made, HT * k + i + 1)
                nc.scalar.activation(ffn_h[:, i, :], (w0, w1)[i % 2][:, :], ACT.Copy).then_inc(gate_kept, 1)

            def silu_gate(k):
                act.wait_ge(gate_kept, HT * (k + 1))
                nc.scalar.activation(ffn_h[:, :, :], ffn_h[:, :, :], ACT.Silu).then_inc(gate_done, 1)

            def norm1(k):
                rstd(k, mv1_done, mv1, lnv1, lnv1_done, rstd1, rstd1_done)

            def norm2(k):
                rstd(k, mv2_done, mv2, lnv2, lnv2_done, rstd2, rstd2_done)

            def exp_and_ln_table():
                nc.scalar.preload_act_table_set("natural_log_exp_and_others")

            exp_and_ln_table()
            act.wait_ge(consts_set, 6)
            norm1(0)
            keep_xT(0, 0)
            act.wait_ge(wT_kept, 7)
            nc.scalar.activation(a_exp[:, :], a_exp[:, :], ACT.Exp).then_inc(a_done, 1)
            norm1(1)
            for i in range(4):
                keep_pre(0, i)
            silu_u(0, 0)
            exp_and_ln_table()
            keep_b(0, 0)
            keep_draw(0, 0)
            keep_draw(0, 1)
            exp_delta(0)
            ln_delta(0)
            keep_xT(1, 1)
            first_part(0, 0)
            second_part(0)
            for i in range(4):
                keep_pre(1, i)
            act.wait_ge(setup_done, 1)
            exps(0, 0)

            def chunk(k, par, has_next, has_after_next, has_previous, has_before_previous):
                for s in range(QUADS):
                    if s == 1 and has_after_next:
                        norm1(k + 2)
                    if s == 2 and has_previous:
                        norm2(k - 1)
                    if s + 1 < QUADS:
                        exps(k, s + 1)
                    elif has_next:
                        exps(k + 1, 0)
                    if s == 0 and has_next:
                        silu_u(k + 1, 1 - par)
                        exp_and_ln_table()
                    if s == 1 and has_next:
                        keep_b(k + 1, 1 - par)
                        keep_draw(k + 1, 0)
                        keep_draw(k + 1, 1)
                        exp_delta(k + 1)
                        ln_delta(k + 1)
                    if s == 2 and has_after_next:
                        keep_xT(k + 2, par)
                    if s == 3 and has_previous:
                        keep_x2T(k - 1)
                        for i in range(HT):
                            keep_gate(k - 1, i)
                        silu_gate(k - 1)
                        exp_and_ln_table()
                    if s == 4:
                        if has_next:
                            first_part(k + 1, 1 - par)
                        if has_after_next:
                            keep_pre(k + 2, 0)
                    if s == 5:
                        if has_after_next:
                            keep_pre(k + 2, 1)
                        if has_next:
                            second_part(k + 1)
                        if has_after_next:
                            keep_pre(k + 2, 2)
                    if s == 7 and has_after_next:
                        keep_pre(k + 2, 3)

            over_chunks(act, chunk)
            norm2(CHUNKS - 1)
            keep_x2T(CHUNKS - 1)
            for i in range(HT):
                keep_gate(CHUNKS - 1, i)
            silu_gate(CHUNKS - 1)

        @block.vector
        def _(dve):
            def scans(k, par, s):
                slot = s % RING
                dve.wait_ge(dbu_done, QUADS * k + s + 1)
                if par and s == 0:
                    dve.wait_ge(carried, QUADS // 2 * (k - par) + QUADS)
                for c in range(CB):
                    start = carry[:, s, c:c + 1] if par else 0.0
                    dve.wait_ge(dA_done, GROUPS * k + CB * s + c + 1)
                    nc.vector.tensor_tensor_scan(h[:, s % 2, c, :], dA[c][:, :], dbu[:, slot, c, :], start,
                                                 ALU.mult, ALU.add).then_inc(scan_done, 1)

            def times_c(k, par, s):
                dve.wait_ge(scan_done, GROUPS * k + CB * (s + 1))
                if not par:
                    nc.vector.tensor_copy(carry[:, s, :], h[:, s % 2, :, T - 1]).then_inc(carried, 1)
                if s == 0:
                    dve.wait_ge(c_made, k + 1)
                if not (isinstance(k, int) and k == 0 and s < 2):
                    dve.wait_ge(sum_done, QUADS * k + s - 1)
                nc.vector.tensor_tensor(hc[:, s % 2, :, :], h[:, s % 2, :, :],
                                        c_bank[:, :].unsqueeze(1).broadcast_to([P, CB, T]), ALU.mult).then_inc(hc_done, 1)

            def gate_y(k, par, i):
                dve.wait_ge(sum_done, QUADS * k + QPT * (i + 1))
                nc.vector.scalar_tensor_tensor(out=y_skip[:, :], in0=u_res[:, par, i, :], scalar=dskip[:, i:i + 1],
                                               in1=y_bank[:, :], op0=ALU.mult, op1=ALU.add).then_inc(skip_done, 1)
                dve.wait_ge(skip_done, DT * k + i + 1)
                if not (isinstance(k, int) and k < 1):
                    dve.wait_ge(mix_made, k)
                nc.vector.tensor_tensor(y_gated[:, i, :], y_skip[:, :], u_res[:, par, DT + i, :], ALU.mult)\
                  .then_inc(y_done, 1)

            def layer_stats(k, x_of, stats, stats_done, mv, mv_done):
                for a in range(TT):
                    nc.vector.bn_stats(stats[:, a, :], x_of(a)).then_inc(stats_done, 1)
                dve.wait_ge(stats_done, TT * (k + 1))
                nc.vector.tensor_copy(stats_seen[:, :], stats[:, TT - 1, 0:1])
                for a in range(TT):
                    last = nc.vector.bn_aggr(mv[:, a, :], stats[:, a, :])
                last.then_inc(mv_done, 1)

            def layer_norm(k, x_of, mv, r, r_done, y, y_done_sem):
                dve.wait_ge(r_done, k + 1)
                for a in range(TT):
                    last = nc.vector.tensor_scalar(y[:, a, :], x_of(a), mv[:, a, 0:1], r[:, a:a + 1],
                                                   ALU.subtract, ALU.mult)
                last.then_inc(y_done_sem, 1)

            def stats_1(k, par):
                dve.wait_ge(x_loaded[par], x_count(k, par))
                if not (isinstance(k, int) and k < 1):
                    dve.wait_ge(norm1_done, k)
                layer_stats(k, lambda a: x_t[:, par, a, :], stats1, stats1_done, mv1, mv1_done)

            def norm_1(k, par):
                if not (isinstance(k, int) and k < 1):
                    dve.wait_ge(xT_made, k)
                layer_norm(k, lambda a: x_t[:, par, a, :], mv1, rstd1, rstd1_done, xn, norm1_done)

            def add_mix(k, par):
                dve.wait_ge(mix_made, k + 1)
                dve.wait_ge(x_reloaded[par], x_count(k, par))
                if not (isinstance(k, int) and k < 1):
                    dve.wait_ge(fin_done, k)
                nc.vector.tensor_tensor(x2[:, :, :], x_again[:, par, :, :],
                                        w0[:, :].rearrange("p (a b) -> p a b", a=TT), ALU.add).then_inc(x2_done, 1)

            def stats_2(k):
                dve.wait_ge(x2_done, k + 1)
                layer_stats(k, lambda a: x2[:, a, :], stats2, stats2_done, mv2, mv2_done)

            def norm_2(k):
                layer_norm(k, lambda a: x2[:, a, :], mv2, rstd2, rstd2_done, x2n, norm2_done)

            def series_factor(k):
                dve.wait_ge(dexp_done, k + 1)
                nc.vector.tensor_scalar(s_dt[:, :, :], e_dt[:, :, :], 1.0 / 3.0, -0.5, ALU.mult, ALU.add)\
                  .then_inc(dfactor_done, 1)

            def softplus(k):
                dve.wait_ge(dsquare_done, k + 1)
                nc.vector.scalar_tensor_tensor(out=s_dt[:, :, :], in0=s_dt[:, :, :], scalar=1.0, in1=e_dt[:, :, :],
                                               op0=ALU.add, op1=ALU.mult).then_inc(dseries_done, 1)
                dve.wait_ge(dseries_done, k + 1)
                dve.wait_ge(dln_done, k + 1)
                nc.vector.tensor_tensor(s_dt[:, :, :], s_dt[:, :, :], a_dt[:, :, :], ALU.min).then_inc(dlog_done, 1)

            def times_up(k, i):
                dve.wait_ge(up_made, HT * k + i + 1)
                if i == 0:
                    dve.wait_ge(gate_done, k + 1)
                nc.vector.tensor_tensor(ffn_h[:, i, :], ffn_h[:, i, :], (w0, w1)[i % 2][:, :], ALU.mult)\
                  .then_inc(ffn_h_done, 1)

            def finish(k, par):
                dve.wait_ge(down_made, k + 1)
                if not (isinstance(k, int) and k < 2):
                    dve.wait_ge(stored[par], x_count(k - 2, par))
                nc.vector.tensor_tensor(fin[:, par, :, :], x2[:, :, :],
                                        w1[:, :].rearrange("p (a b) -> p a b", a=TT), ALU.add).then_inc(fin_done, 1)

            stats_1(0, 0)
            norm_1(0, 0)
            dve.wait_ge(weights_in, 16 * LOADS)
            for i in range(DT):
                for tap in range(TAPS):
                    nc.vector.tensor_scalar(w_rows[:, CONV + TAPS * i + tap, :], w_in_rows[:, i, :],
                                            conv_w[:, i, tap:tap + 1], None, ALU.mult).then_inc(w_scaled, 1)
            nc.vector.tensor_scalar(w_rows[:, GW:NW, :], w_int[:, :, :], SCALE, None, ALU.mult).then_inc(w_scaled, 1)
            for i in range(6):
                dve.wait_ge(wT_made, i + 1)
                nc.vector.tensor_copy(wT[:, 4 * i:4 * i + 4, :].rearrange("p a b -> p (a b)"), banks[i][:, :])\
                  .then_inc(wT_kept, 1)
            dve.wait_ge(wT_made, 7)
            nc.vector.tensor_copy(wT[:, NW - 1, :], banks[6][:, 0:P])
            nc.vector.tensor_copy(a_exp[:, :], banks[6][:, P:P + GROUPS]).then_inc(wT_kept, 1)
            dve.wait_ge(wT_made, 8)
            nc.vector.tensor_copy(rep[:, :, :].rearrange("p a b -> p (a b)"), banks[7][0:PARTS * 32, :]).then_inc(wT_kept, 1)
            dve.wait_ge(wdelta_made, 1)
            nc.vector.tensor_copy(w_delta[:, :, :].rearrange("p a b -> p (a b)"), banks[0][:, :]).then_inc(wT_kept, 1)
            dve.wait_ge(a_done, 1)
            nc.vector.tensor_scalar(a_neg[:, :], a_exp[:, :], -1.0, None, ALU.mult).then_inc(setup_done, 1)
            stats_1(1, 1)
            norm_1(1, 1)
            series_factor(0)
            softplus(0)

            def chunk(k, par, has_next, has_after_next, has_previous, has_before_previous):
                for s in range(QUADS):
                    scans(k, par, s)
                    if s == 0 and has_previous:
                        gate_y(k - 1, 1 - par, 1)
                    times_c(k, par, s)
                    if s == 4:
                        gate_y(k, par, 0)
                    if s == 0:
                        if has_before_previous:
                            finish(k - 2, par)
                        if has_after_next:
                            stats_1(k + 2, par)
                    if s == 1:
                        if has_previous:
                            add_mix(k - 1, 1 - par)
                            stats_2(k - 1)
                        if has_after_next:
                            norm_1(k + 2, par)
                    if s == 2:
                        if has_next:
                            series_factor(k + 1)
                        if has_previous:
                            norm_2(k - 1)
                    if s == 3 and has_next:
                        softplus(k + 1)
                    if s == 6 and has_previous:
                        times_up(k - 1, 0)
                        times_up(k - 1, 1)
                    if s == 7 and has_previous:
                        times_up(k - 1, 2)

            over_chunks(dve, chunk)
            last = CHUNKS - 1
            gate_y(last, 1, 1)
            finish(last - 1, 0)
            add_mix(last, 1)
            stats_2(last)
            norm_2(last)
            for i in range(HT):
                times_up(last, i)
            finish(last, 1)

        @block.tensor
        def _(pe):
            def bank_free(sem_, n):
                pe.wait_ge(sem_, n)

            def transpose_x(k):
                pe.wait_ge(norm1_done, k + 1)
                for a in range(TT):
                    last = nc.tensor.transpose(w0[:, P * a:P * a + P], xn[:, a, :], ident[:, :])
                last.then_inc(xT_made, 1)

            def project_pre(k, par, i):
                if i == 0:
                    pe.wait_ge(xT_kept, k + 1)
                bank = (w1, w0, w1, w1)[i]
                at = T * par
                if i < DT:
                    for tap in range(TAPS):
                        last = nc.tensor.matmul(bank[:, :], wT[:, CONV + TAPS * i + tap, :], xT[:, at + tap:at + tap + T],
                                                start=(tap == 0), stop=(tap == TAPS - 1))
                else:
                    last = nc.tensor.matmul(bank[:, :], wT[:, RES + i - DT, :], xT[:, at + HALO:at + HALO + T],
                                            start=True, stop=True)
                last.then_inc(pre_made, 1)

            def project_b(k, par):
                pe.wait_ge(u_done, k + 1)
                for i in range(DT):
                    last = nc.tensor.matmul(w1[:, :], wT[:, BW + i, :], u_res[:, par, i, :],
                                            start=(i == 0), stop=(i == DT - 1))
                last.then_inc(b_made, 1)

            def project_delta(k, par, i):
                for j in range(DT):
                    last = nc.tensor.matmul((w0, w1)[i][:, :], w_delta[:, j, P * i:P * i + P], u_res[:, par, j, :],
                                            start=(j == 0), stop=(j == DT - 1))
                last.then_inc(draw_made, 1)

            def project_c(k, par):
                if not (isinstance(k, int) and k == 0):
                    pe.wait_ge(hc_done, QUADS * k)
                for i in range(DT):
                    last = nc.tensor.matmul(c_bank[:, :], wT[:, CW + i, :], u_res[:, par, i, :],
                                            start=(i == 0), stop=(i == DT - 1))
                last.then_inc(c_made, 1)

            def spread_delta(k, par, s):
                tile, sub = s // QPT, s % QPT
                if s == 0:
                    pe.wait_ge(stacked[par], stack_count(k, par))
                for c in range(CB):
                    if not (isinstance(k, int) and k == 0 and s == 0):
                        pe.wait_ge(scan_done, GROUPS * k + CB * (s - 1) + c + 1)
                    nc.tensor.matmul(dA[c][:, :], rep[:, sub, :], stack[:, par, c, tile, :],
                                     start=True, stop=True).then_inc(delta_spread, 1)

            def sum_states(k, s):
                sub = s % QPT
                pe.wait_ge(hc_done, QUADS * k + s + 1)
                if sub == 0 and not (isinstance(k, int) and k == 0 and s == 0):
                    pe.wait_ge(skip_done, DT * k + s // QPT)
                for c in range(CB):
                    last = nc.tensor.matmul(y_bank[32 * c:32 * c + 32, :], sel[:, sub, 0, :], hc[:, s % 2, c, :],
                                            start=(sub == 0), stop=(sub == QPT - 1))
                last.then_inc(sum_done, 1)

            def project_mix(k):
                pe.wait_ge(y_done, DT * (k + 1))
                for a in range(TT):
                    for i in range(DT):
                        last = nc.tensor.matmul(w0[:, P * a:P * a + P], y_gated[:, i, P * a:P * a + P], wT[:, OW + i, :],
                                                start=(i == 0), stop=(i == DT - 1))
                last.then_inc(mix_made, 1)

            def transpose_x2(k):
                pe.wait_ge(norm2_done, k + 1)
                for a in range(TT):
                    last = nc.tensor.transpose(w1[:, P * a:P * a + P], x2n[:, a, :], ident[:, :])
                last.then_inc(x2T_made, 1)

            def project_gate(k, i):
                if i == 0:
                    pe.wait_ge(x2T_kept, k + 1)
                nc.tensor.matmul((w0, w1)[i % 2][:, :], wT[:, GW + i, :], x2T[:, :], start=True, stop=True)\
                  .then_inc(gate_made, 1)

            def project_up(k, i):
                nc.tensor.matmul((w0, w1)[i % 2][:, :], wT[:, UW + i, :], x2T[:, :], start=True, stop=True)\
                  .then_inc(up_made, 1)

            def project_down(k):
                pe.wait_ge(ffn_h_done, HT * (k + 1))
                for a in range(TT):
                    for i in range(HT):
                        last = nc.tensor.matmul(w1[:, P * a:P * a + P], ffn_h[:, i, P * a:P * a + P], wT[:, DW + i, :],
                                                start=(i == 0), stop=(i == HT - 1))
                last.then_inc(down_made, 1)

            pe.wait_ge(consts_set, 6)
            transpose_x(0)
            pe.wait_ge(weights_in, 16 * LOADS)
            pe.wait_ge(w_scaled, DT * TAPS + 1)
            for i in range(6):
                for j in range(4):
                    last = nc.tensor.transpose(banks[i][:, P * j:P * j + P], w_rows[:, 4 * i + j, :], ident[:, :])
                last.then_inc(wT_made, 1)
            bank_free(xT_kept, 1)
            nc.tensor.transpose(banks[6][:, 0:P], w_rows[:, NW - 1, :], ident[:, :])
            nc.tensor.transpose(banks[6][:, P:P + GROUPS], alog_rows[:, :], ident[0:GROUPS, 0:GROUPS]).then_inc(wT_made, 1)
            for q in range(QPT):
                last = nc.tensor.transpose(banks[7][0:PARTS * 32, P * q:P * q + P],
                                           sel[:, q, :, :].rearrange("p a b -> p (a b)"), ident[:, :])
            last.then_inc(wT_made, 1)
            pe.wait_ge(wT_kept, 1)
            for i in range(DT):
                last = nc.tensor.matmul(banks[0][:, DI * i:DI * i + DI], wx_dt[:, P * i:P * i + P], wdt_T[:, :],
                                        start=True, stop=True)
            last.then_inc(wdelta_made, 1)
            pe.wait_ge(wT_kept, 9)
            project_pre(0, 0, 0)
            project_pre(0, 0, 1)
            bank_free(pre_kept, 1)
            project_pre(0, 0, 2)
            bank_free(pre_kept, 3)
            project_pre(0, 0, 3)
            project_b(0, 0)
            project_delta(0, 0, 0)
            bank_free(b_kept, 1)
            project_delta(0, 0, 1)
            project_c(0, 0)
            bank_free(dkept, 1)
            transpose_x(1)
            bank_free(dkept, 2)
            project_pre(1, 1, 0)
            project_pre(1, 1, 1)
            bank_free(pre_kept, 5)
            project_pre(1, 1, 2)
            bank_free(pre_kept, 7)
            project_pre(1, 1, 3)
            spread_delta(0, 0, 0)

            def chunk(k, par, has_next, has_after_next, has_previous, has_before_previous):
                nxt = 1 - par
                for s in range(QUADS):
                    if s > 0:
                        sum_states(k, s - 1)
                    if s + 1 < QUADS:
                        spread_delta(k, par, s + 1)
                    elif has_next:
                        spread_delta(k + 1, nxt, 0)
                    if s == 0 and has_previous:
                        project_mix(k - 1)
                    if s == 1 and has_next:
                        if has_before_previous:
                            bank_free(fin_done, k - 1)
                        project_b(k + 1, nxt)
                        if has_previous:
                            bank_free(x2_done, k)
                        project_delta(k + 1, nxt, 0)
                        bank_free(b_kept, k + 2)
                        project_delta(k + 1, nxt, 1)
                    if s == 2:
                        if has_after_next:
                            bank_free(dkept, DT * (k + 1) + 1)
                            transpose_x(k + 2)
                        if has_previous:
                            if has_next:
                                bank_free(dkept, DT * (k + 2))
                            else:
                                bank_free(fin_done, k - 1)
                            transpose_x2(k - 1)
                    if s == 3 and has_previous:
                        if has_after_next:
                            bank_free(xT_kept, k + 3)
                        elif has_next:
                            bank_free(dkept, DT * (k + 1) + 1)
                        else:
                            bank_free(x2_done, k)
                        project_gate(k - 1, 0)
                        project_gate(k - 1, 1)
                        bank_free(gate_kept, HT * (k - 1) + 1)
                        project_gate(k - 1, 2)
                    if s == 4 and has_after_next:
                        if has_previous:
                            bank_free(gate_kept, HT * (k - 1) + 2)
                        else:
                            bank_free(dkept, DT * (k + 2))
                        project_pre(k + 2, par, 0)
                        if has_previous:
                            bank_free(gate_kept, HT * k)
                        project_pre(k + 2, par, 1)
                    if s == 5:
                        if has_after_next:
                            bank_free(pre_kept, 4 * (k + 2) + 1)
                            project_pre(k + 2, par, 2)
                        if has_previous:
                            if has_after_next:
                                bank_free(pre_kept, 4 * (k + 2) + 2)
                            else:
                                bank_free(gate_kept, HT * k)
                            project_up(k - 1, 0)
                            if has_after_next:
                                bank_free(pre_kept, 4 * (k + 2) + 3)
                            project_up(k - 1, 1)
                    if s == 7:
                        if has_previous:
                            bank_free(ffn_h_done, HT * (k - 1) + 1)
                            project_up(k - 1, 2)
                        if has_after_next:
                            if has_previous:
                                bank_free(ffn_h_done, HT * (k - 1) + 2)
                            else:
                                bank_free(pre_kept, 4 * (k + 2) + 3)
                            project_pre(k + 2, par, 3)
                        sum_states(k, QUADS - 1)
                        if has_next:
                            project_c(k + 1, nxt)
                        if has_previous:
                            if has_after_next:
                                bank_free(pre_kept, 4 * (k + 3))
                            project_down(k - 1)

            over_chunks(pe, chunk)
            last_k = CHUNKS - 1
            project_mix(last_k)
            bank_free(fin_done, last_k)
            transpose_x2(last_k)
            bank_free(x2_done, CHUNKS)
            project_gate(last_k, 0)
            project_gate(last_k, 1)
            bank_free(gate_kept, HT * last_k + 1)
            project_gate(last_k, 2)
            bank_free(gate_kept, HT * CHUNKS)
            project_up(last_k, 0)
            project_up(last_k, 1)
            bank_free(ffn_h_done, HT * last_k + 1)
            project_up(last_k, 2)
            project_down(last_k)


_INS = ['L0_attn_x', 'L0_attn_W_in', 'L0_attn_W_conv', 'L0_attn_b_conv', 'L0_attn_W_xproj', 'L0_attn_W_dt',
        'L0_attn_b_dt', 'L0_attn_A_log', 'L0_attn_D', 'L0_attn_W_out', 'L0_ffn_w_gate', 'L0_ffn_w_up', 'L0_ffn_w_down']
_OUT_SHAPE = (8, 1024, 128)


def kernel(**inputs):
    import numpy as _np
    import concourse.bacc as _bacc
    from concourse import mybir as _mybir
    from concourse.bass_utils import run_bass_kernel_spmd as _run

    nc = _bacc.Bacc("TRN2", target_bir_lowering=False, num_devices=1)
    arrays, args = {}, []
    for name in _INS:
        a = _np.ascontiguousarray(inputs[name])
        arrays[f"in_{name}"] = a
        args.append(nc.dram_tensor(f"in_{name}", a.shape, _mybir.dt.from_np(a.dtype), kind="ExternalInput").ap())
    args.append(nc.dram_tensor("out_0", _OUT_SHAPE, _mybir.dt.float32, kind="ExternalOutput").ap())
    mamba_block_and_gated_ffn(nc, *args)
    r = _run(nc, [arrays], core_ids=[0])
    return r.results[0]["out_0"]
```
